# Optimizing a Trainium2 kernel written in Bass

```python
import numpy as np
import jax
import jax.numpy as jnp

def _softmax(x, axis=-1):
    return jax.nn.softmax(x, axis=axis)

def _gelu(x):
    return jax.nn.gelu(x, approximate=True)

def _silu(x):
    return jax.nn.silu(x)

def _sigmoid(x):
    return jax.nn.sigmoid(x)

def _layernorm(x, axis=-1, eps=1e-05):
    m = jnp.mean(x, axis=axis, keepdims=True)
    v = jnp.var(x, axis=axis, keepdims=True)
    return (x - m) / jnp.sqrt(v + eps)

def _scatter_add(tgt, idx, src, axis=0):
    return tgt.at[idx].add(src)

def _segment_sum(src, seg, n):
    return jax.ops.segment_sum(src, seg, n)
kernel_name = 'mk_adj_resnorm_d2_adj_r2_6cdda7'

def setup_inputs(seed: int=0):
    np.random.seed(seed)
    _w = jnp.asarray

    def _rec_inputs():
        import jax
        import jax.numpy as jnp
        _gk = jax.random.key(seed)
        x = -0.0002928 + 1 * jax.random.normal(jax.random.fold_in(_gk, 1), (16, 512, 128), jnp.float32)
        _w = (1.0 + jnp.arange(512, dtype=jnp.float32)) ** (-0.5)
        _w = _w / _w.mean()
        _pij = jnp.clip(0.00390625 * _w[:, None] * _w[None, :], 0.0, 1.0)
        _a = jax.random.uniform(jax.random.fold_in(_gk, 2), (16, 512, 512)) < _pij
        _a = jnp.logical_or(_a, jnp.swapaxes(_a, -1, -2))
        _a = jnp.logical_or(_a, jnp.eye(512, dtype=bool))
        _af = _a.astype(jnp.float32)
        _af = _af * jax.random.uniform(jax.random.fold_in(_gk, 3), (16, 512, 512), jnp.float32, 0.05, 1)
        adj = _af
        return (x, adj)
    x, adj = _rec_inputs()

    def _L0_gnn_setup():
        import jax, jax.numpy as jnp
        import numpy as np
        IN_DIM = 128
        OUT_DIM = 128
        key = jax.random.key(seed)
        k1, k2, k3, k4 = jax.random.split(key, 4)
        B, N = (8, 1024)
        X = jax.random.normal(k1, (B, N, IN_DIM), dtype=jnp.float32)
        adj = jax.random.uniform(k2, (B, N, N), dtype=jnp.float32)
        bound = 1.0 / np.sqrt(IN_DIM)
        W = jax.random.uniform(k3, (OUT_DIM, IN_DIM), minval=-bound, maxval=bound, dtype=jnp.float32)
        b = jax.random.uniform(k4, (OUT_DIM,), minval=-bound, maxval=bound, dtype=jnp.float32)
        return {'X': X, 'adj': adj, 'W': W, 'b': b}
    _L0_gnn_all = _L0_gnn_setup()
    _L0_gnn_in = {k: v for k, v in _L0_gnn_all.items() if k in ('W', 'b')}
    del _L0_gnn_all

    def _L1_gnn_setup():
        import jax, jax.numpy as jnp
        import numpy as np
        from jax import lax
        DIM = 128
        EPS = 1e-05

        def _bn(h, g, b, m, v):
            scale = g / jnp.sqrt(v + EPS)
            return h * scale[None, :, None] + (b - m * scale)[None, :, None]

        def _conv1d(h, w, pad):
            return lax.conv_general_dilated(h, w, window_strides=(1,), padding=[(pad, pad)], dimension_numbers=('NCH', 'OIH', 'NCH'))
        key = jax.random.key(seed)
        ks = jax.random.split(key, 16)
        bs, n, d = (16, 1024, DIM)
        s = 0.05
        return {'x': jax.random.normal(ks[0], (bs, n, d), jnp.float32), 'mask': jnp.ones((bs, n, n), jnp.float32), 'w_se': jax.random.normal(ks[1], (3, d), jnp.float32) * s, 'b_se': jnp.zeros((3,), jnp.float32), 'conv1_w': jax.random.normal(ks[2], (d, d, 1), jnp.float32) * s, 'bn1_g': jnp.ones((d,), jnp.float32), 'bn1_b': jnp.zeros((d,), jnp.float32), 'bn1_m': jnp.zeros((d,), jnp.float32), 'bn1_v': jnp.ones((d,), jnp.float32), 'conv2_w': jax.random.normal(ks[3], (d, d, 17), jnp.float32) * s, 'bn2_g': jnp.ones((d,), jnp.float32), 'bn2_b': jnp.zeros((d,), jnp.float32), 'bn2_m': jnp.zeros((d,), jnp.float32), 'bn2_v': jnp.ones((d,), jnp.float32), 'w_msg': jax.random.normal(ks[4], (d, d), jnp.float32) * s, 'b_msg': jnp.zeros((d,), jnp.float32), 'w_ih': jax.random.normal(ks[5], (3 * d, 2 * d), jnp.float32) * s, 'b_ih': jnp.zeros((3 * d,), jnp.float32), 'w_hh': jax.random.normal(ks[6], (3 * d, d), jnp.float32) * s, 'b_hh': jnp.zeros((3 * d,), jnp.float32)}
    _L1_gnn_all = _L1_gnn_setup()
    _L1_gnn_in = {k: v for k, v in _L1_gnn_all.items() if k in ('w_se', 'b_se', 'conv1_w', 'bn1_g', 'bn1_b', 'bn1_m', 'bn1_v', 'conv2_w', 'bn2_g', 'bn2_b', 'bn2_m', 'bn2_v', 'w_msg', 'b_msg', 'w_ih', 'b_ih', 'w_hh', 'b_hh')}
    del _L1_gnn_all
    return {'x': x, 'adj': adj, 'L0_gnn_W': _L0_gnn_in['W'], 'L0_gnn_b': _L0_gnn_in['b'], 'L1_gnn_w_se': _L1_gnn_in['w_se'], 'L1_gnn_b_se': _L1_gnn_in['b_se'], 'L1_gnn_conv1_w': _L1_gnn_in['conv1_w'], 'L1_gnn_bn1_g': _L1_gnn_in['bn1_g'], 'L1_gnn_bn1_b': _L1_gnn_in['bn1_b'], 'L1_gnn_bn1_m': _L1_gnn_in['bn1_m'], 'L1_gnn_bn1_v': _L1_gnn_in['bn1_v'], 'L1_gnn_conv2_w': _L1_gnn_in['conv2_w'], 'L1_gnn_bn2_g': _L1_gnn_in['bn2_g'], 'L1_gnn_bn2_b': _L1_gnn_in['bn2_b'], 'L1_gnn_bn2_m': _L1_gnn_in['bn2_m'], 'L1_gnn_bn2_v': _L1_gnn_in['bn2_v'], 'L1_gnn_w_msg': _L1_gnn_in['w_msg'], 'L1_gnn_b_msg': _L1_gnn_in['b_msg'], 'L1_gnn_w_ih': _L1_gnn_in['w_ih'], 'L1_gnn_b_ih': _L1_gnn_in['b_ih'], 'L1_gnn_w_hh': _L1_gnn_in['w_hh'], 'L1_gnn_b_hh': _L1_gnn_in['b_hh']}

def reference(x, adj, L0_gnn_W, L0_gnn_b, L1_gnn_w_se, L1_gnn_b_se, L1_gnn_conv1_w, L1_gnn_bn1_g, L1_gnn_bn1_b, L1_gnn_bn1_m, L1_gnn_bn1_v, L1_gnn_conv2_w, L1_gnn_bn2_g, L1_gnn_bn2_b, L1_gnn_bn2_m, L1_gnn_bn2_v, L1_gnn_w_msg, L1_gnn_b_msg, L1_gnn_w_ih, L1_gnn_b_ih, L1_gnn_w_hh, L1_gnn_b_hh):
    import jax
    import jax.numpy as jnp

    def _L0_gnn_ref(X, adj, W, b):
        import jax, jax.numpy as jnp
        import numpy as np
        IN_DIM = 128
        OUT_DIM = 128
        N = adj.shape[-1]
        adj_hat = adj + jnp.eye(N, dtype=adj.dtype)
        d = jnp.sum(adj_hat, axis=-1) ** (-0.5)
        adj_norm = d[..., :, None] * adj_hat * d[..., None, :]
        H = jnp.matmul(adj_norm, X)
        out = jnp.einsum('bnf,of->bno', H, W) + b
        return jax.nn.relu(out)

    def _L1_gnn_ref(x, mask, w_se, b_se, conv1_w, bn1_g, bn1_b, bn1_m, bn1_v, conv2_w, bn2_g, bn2_b, bn2_m, bn2_v, w_msg, b_msg, w_ih, b_ih, w_hh, b_hh):
        import jax, jax.numpy as jnp
        import numpy as np
        from jax import lax
        DIM = 128
        EPS = 1e-05

        def _bn(h, g, b, m, v):
            scale = g / jnp.sqrt(v + EPS)
            return h * scale[None, :, None] + (b - m * scale)[None, :, None]

        def _conv1d(h, w, pad):
            return lax.conv_general_dilated(h, w, window_strides=(1,), padding=[(pad, pad)], dimension_numbers=('NCH', 'OIH', 'NCH'))
        d = x.shape[-1]
        xc = jnp.transpose(x, (0, 2, 1))
        h = _bn(_conv1d(xc, conv1_w, 0), bn1_g, bn1_b, bn1_m, bn1_v)
        h = jax.nn.relu(h)
        h = _bn(_conv1d(h, conv2_w, 8), bn2_g, bn2_b, bn2_m, bn2_v)
        x_conv = jnp.transpose(jax.nn.relu(h + xc), (0, 2, 1))
        s = x @ w_se.T + b_se
        sq = jnp.sum(s * s, axis=-1)
        dist = sq[:, :, None] + sq[:, None, :] - 2.0 * jnp.einsum('bnd,bmd->bnm', s, s)
        A = jnp.exp(-dist) * mask
        msg = jax.nn.relu(x @ w_msg.T + b_msg)
        x_nmp = jnp.einsum('bnm,bmd->bnd', A, msg)
        x_in = jnp.concatenate([x_conv, x_nmp], axis=-1)
        gi = x_in @ w_ih.T + b_ih
        gh = x @ w_hh.T + b_hh
        gi_r, gi_z, gi_n = (gi[..., :d], gi[..., d:2 * d], gi[..., 2 * d:])
        gh_r, gh_z, gh_n = (gh[..., :d], gh[..., d:2 * d], gh[..., 2 * d:])
        r = jax.nn.sigmoid(gi_r + gh_r)
        z = jax.nn.sigmoid(gi_z + gh_z)
        nn_ = jnp.tanh(gi_n + r * gh_n)
        return (1.0 - z) * nn_ + z * x
    x = _layernorm(x + _L0_gnn_ref(x, adj, L0_gnn_W, L0_gnn_b), axis=-1)
    x = _layernorm(x + _L1_gnn_ref(x, adj, L1_gnn_w_se, L1_gnn_b_se, L1_gnn_conv1_w, L1_gnn_bn1_g, L1_gnn_bn1_b, L1_gnn_bn1_m, L1_gnn_bn1_v, L1_gnn_conv2_w, L1_gnn_bn2_g, L1_gnn_bn2_b, L1_gnn_bn2_m, L1_gnn_bn2_v, L1_gnn_w_msg, L1_gnn_b_msg, L1_gnn_w_ih, L1_gnn_b_ih, L1_gnn_w_hh, L1_gnn_b_hh), axis=-1)
    return x

_drawn_inputs = setup_inputs


def setup_inputs(seed=0):
    import zlib

    import numpy as np

    out = dict(_drawn_inputs(seed))
    spreads = {'L1_gnn_b_se': (0.0, 0.8),
     'L1_gnn_bn1_g': (1.0, 0.6),
     'L1_gnn_bn1_b': (0.0, 0.416),
     'L1_gnn_bn1_m': (0.0, 0.378),
     'L1_gnn_bn1_v': (1.0, 0.6),
     'L1_gnn_bn2_g': (1.0, 0.578),
     'L1_gnn_bn2_b': (0.0, 0.744),
     'L1_gnn_bn2_m': (0.0, 0.574),
     'L1_gnn_bn2_v': (1.0, 0.6),
     'L1_gnn_b_msg': (0.0, 0.605),
     'L1_gnn_b_ih': (0.0, 0.27),
     'L1_gnn_b_hh': (0.0, 0.398)}
    factors = {}
    for name, (base, spread) in spreads.items():
        noise = np.random.default_rng([zlib.crc32(name.encode()), seed]).standard_normal(out[name].shape)
        drawn = base * np.exp(spread * noise) if base else spread * noise
        out[name] = jnp.asarray(drawn.astype(out[name].dtype))
    for name, factor in factors.items():
        out[name] = (out[name] * factor).astype(out[name].dtype)
    return out
```

```python
from contextlib import ExitStack

import concourse.bass as bass
from concourse import mybir

FP32 = mybir.dt.float32
FP32R = mybir.dt.float32r
ACT = mybir.ActivationFunctionType
ALU = mybir.AluOpType

G, N, D, TAPS, SE = 16, 512, 128, 17, 3
P = 128
NB = N // P
PAIRS = G // 2
HALO = TAPS // 2
EPS = 1e-5
DIST_ROWS = 8 * SE


def distance_factors():
    import numpy as np
    hi, lo, minus = (1, 0, 0), (-1, 1, 0), (0, 0, -1)
    twice = lambda f: tuple(2 * x for x in f)
    kinds = [(0, hi, twice(hi)), (0, lo, twice(hi)), (0, hi, twice(lo)), (0, lo, twice(lo)),
             (1, hi, minus), (1, lo, minus), (1, minus, hi), (1, minus, lo)]
    f = np.zeros((P, 8), np.float32)
    for i, (square, moving, stationary) in enumerate(kinds):
        f[SE * i:SE * (i + 1)] = (square, 1 - square) + moving + stationary
    return f


def after(pair, slot):
    return pair * 2 + (slot + 1)


def loaded(pair):
    return (pair + 1) * 16


def gnn_kernel(nc, t, out):
    ctx = ExitStack()
    with ctx:
        def sb(name, shape, dt=FP32):
            return ctx.enter_context(nc.sbuf_tensor(name, shape, dt))

        def sem(name):
            return ctx.enter_context(nc.semaphore(name))

        ident = sb("ident", [P, P])
        coef = sb("coef", [P, 8])
        w0T = sb("w0T", [P, D])
        b0_rep = sb("b0_rep", [P, D])
        bmsg_rep = sb("bmsg_rep", [P, D])
        wmsgT = sb("wmsgT", [P, D])
        wseT = sb("wseT", [P, SE])
        wse_rep = sb("wse_rep", [P, P])
        bse_col = sb("bse_col", [P, 1])
        bse_lin = sb("bse_lin", [P, 1])
        w1h, w1l = sb("w1h", [P, D], FP32R), sb("w1l", [P, D], FP32R)
        w2h, w2l = sb("w2h", [P, TAPS, D], FP32R), sb("w2l", [P, TAPS, D], FP32R)
        wihh, wihl = sb("wihh", [P, 2, 3 * D], FP32R), sb("wihl", [P, 2, 3 * D], FP32R)
        whhh, whhl = sb("whhh", [P, 3 * D], FP32R), sb("whhl", [P, 3 * D], FP32R)
        wseh, wsel = sb("wseh", [P, P], FP32R), sb("wsel", [P, P], FP32R)
        bn = sb("bn", [P, 8])
        bn_fac = sb("bn_fac", [P, 4])
        bn_tmp = sb("bn_tmp", [P, 4])
        bih, bhh = sb("bih", [P, 3]), sb("bhh", [P, 3])
        gbias2 = sb("gbias2", [P, 2])
        neg_half = sb("neg_half", [P, NB])
        gbias = sb("gbias", [P, 2])

        def two(name, shape, dt=FP32):
            return [sb(f"{name}{s}", shape, dt) for s in range(2)]

        adjT = two("adjT", [P, NB, N])
        adjN = two("adjN", [P, NB, N])
        xT = two("xT", [P, N])
        xN = two("xN", [P, NB, D])
        deg = two("deg", [P, NB])
        dinv = two("dinv", [P, NB])
        yd = two("yd", [P, NB, D])
        z1 = z2 = z3 = y0 = x1N = two("x1N", [P, NB, D])
        stats = two("stats", [P, NB, 6])
        mv = two("mv", [P, NB, 2])
        rstd = two("rstd", [P, NB])
        x1T = two("x1T", [P, N])
        x1h, x1l = two("x1h", [P, N], FP32R), two("x1l", [P, N], FP32R)
        hT = two("hT", [P, N])
        hh = two("hh", [P, N + 2 * HALO], FP32R)
        hl = two("hl", [P, N + 2 * HALO], FP32R)
        sqr = su = suL = two("suL", [P, N])
        slin = suR = two("suR", [P, N])
        suh = two("suh", [P, N], FP32R)
        dR, dL = two("dR", [P, N], FP32R), two("dL", [P, N], FP32R)
        mb_ = msg = two("msg", [P, NB, D])
        em_both = sb("em", [P, 2, NB, N])
        em = [em_both[:, s] for s in range(2)]
        gc = xcT = two("xcT", [P, N])
        xch, xcl = two("xch", [P, N], FP32R), two("xcl", [P, N], FP32R)
        nmh, nml = two("nmh", [P, N], FP32R), two("nml", [P, N], FP32R)
        tr = tr1 = q1 = q2 = nT = two("nT", [P, N])
        tz = two("tz", [P, N])
        e1 = e2 = y1 = two("y1", [P, N])
        e3 = two("e3", [P, N])
        stats1 = two("stats1", [P, NB, 6])
        mv1 = two("mv1", [P, NB, 2])
        rstd1 = two("rstd1", [P, NB])
        outN = two("outN", [P, NB, D])

        at, parts = 0, []
        for width in (TAPS * D, 2 * 3 * D, 3 * D, D):
            parts.append(em_both[:].rearrange("p s b n -> p (s b n)")[:, at:at + width])
            at += width
        w2, wih = parts[0].rearrange("p (k o) -> p k o", k=TAPS), parts[1].rearrange("p (k o) -> p k o", k=2)
        whh, w1 = parts[2], parts[3]

        ps = ctx.enter_context(nc.psum_tensor("ps", [P, 8, N], FP32))

        def bank(i):
            return ps[:, i, :]

        w_in = sem("w_in")
        w_hi, w_lo = sem("w_hi"), sem("w_lo")
        rep_ok, fold_ok, fold_step = sem("rep_ok"), sem("fold_ok"), sem("fold_step")
        half_ok, fold_var, fold_pow = sem("half_ok"), sem("fold_var"), sem("fold_pow")
        halo_ok, bse_zero = sem("halo_ok"), sem("bse_zero")
        adjT_in = [sem(f"adjT_in{s}") for s in range(2)]
        adjN_in = [sem(f"adjN_in{s}") for s in range(2)]
        xT_in = [sem(f"xT_in{s}") for s in range(2)]
        xN_in = [sem(f"xN_in{s}") for s in range(2)]
        out_stored = [sem(f"out_stored{s}") for s in range(2)]
        (deg_ok, deg1_ok, dinv_ok, y_mm, yd_ok, l0_mm, z1_ok, z2_ok, z3_ok, y0_ok, st_ok, mv_ok, rs_ok, rstd_ok, x1N_ok,
         x1_mm, x1T_ok, x1h_ok, x1l_ok, c1_mm, h_ok, hh_ok, hl_ok, s_mm, sqr_ok, slin_ok, su_ok, suh_ok, suR_ok,
         suL_ok, dR_ok, dL_ok, msg_mm, mb_ok, msg_ok, dist_mm, exp_ok, em_ok, c2_mm, gc_ok, xc_ok, xch_ok, xcl_ok,
         nm_mm, nmh_ok, nml_ok, r_mm, z_mm, hn_mm, in_mm, tr_ok, tz_ok, tr1_ok, q1_ok, q2_ok, n_ok, e1_ok, e2_ok,
         e3_ok, y1_ok, y1_mm, st1_ok, mv1_ok, rs1_ok, rstd1_ok, out_ok) = (sem(x) for x in (
            "deg_ok deg1_ok dinv_ok y_mm yd_ok l0_mm z1_ok z2_ok z3_ok y0_ok st_ok mv_ok rs_ok rstd_ok x1N_ok "
            "x1_mm x1T_ok x1h_ok x1l_ok c1_mm h_ok hh_ok hl_ok s_mm sqr_ok slin_ok su_ok suh_ok suR_ok "
            "suL_ok dR_ok dL_ok msg_mm mb_ok msg_ok dist_mm exp_ok em_ok c2_mm gc_ok xc_ok xch_ok xcl_ok "
            "nm_mm nmh_ok nml_ok r_mm z_mm hn_mm in_mm tr_ok tz_ok tr1_ok q1_ok q2_ok n_ok e1_ok e2_ok "
            "e3_ok y1_ok y1_mm st1_ok mv1_ok rs1_ok rstd1_ok out_ok").split())

        weight_dmas = [
            (ident[:], t["ident"]), (coef[:], t["coef"]), (w0T[:], t["w0T"]), (wmsgT[:], t["wmsgT"]),
            (wseT[:], t["wseT"]), (w1, t["w1T"]), (w2, t["w2T"]),
            (wih[:, 0, :], t["wihT"][0:P, :]), (wih[:, 1, :], t["wihT"][P:2 * P, :]), (whh, t["whhT"]),
            (b0_rep[:], t["b0"].partition_broadcast(P)), (bmsg_rep[:], t["bmsg"].partition_broadcast(P)),
            (bih[:], t["bih"]), (bhh[:], t["bhh"]),
        ]
        weight_dmas.append((bn[:], t["bn"]))
        for i in range(DIST_ROWS // SE):
            weight_dmas.append((bse_col[SE * i:SE * (i + 1), :], t["bse"].rearrange("(p a) -> p a", a=1)))
        WEIGHTS_IN = 16 * len(weight_dmas)

        block = ctx.enter_context(nc.Block())

        def pair_loop(eng, first, body, last):
            first(0)
            with eng.Fori(1, PAIRS - 1) as pair:
                body(pair)
            last(PAIRS - 1)

        @block.sync
        def _(sync):
            def load(pair, s, reuse):
                g = pair * 2 + s
                if reuse:
                    sync.wait_ge(em_ok, after(pair - 1, s))
                sync.dma_start(adjT[s][:], t["adjT"][bass.ds(g, 1)].rearrange("a (b p) n -> p (a b) n", p=P)).then_inc(adjT_in[s], 16)
                if reuse:
                    sync.wait_ge(deg_ok, after(pair - 1, s))
                    sync.wait_ge(y_mm, after(pair - 1, s))
                    sync.wait_ge(y0_ok, after(pair - 1, s))
                sync.dma_start(xT[s][:], t["xT"][bass.ds(g, 1)].rearrange("a p n -> p (a n)")).then_inc(xT_in[s], 16)
                sync.dma_start(adjN[s][:], t["adjN"][bass.ds(g, 1)].rearrange("a (b p) n -> p (a b) n", p=P)).then_inc(adjN_in[s], 16)
                sync.dma_start(xN[s][:], t["xN"][bass.ds(g, 1)].rearrange("a (b p) n -> p (a b) n", p=P)).then_inc(xN_in[s], 16)

            def store(pair, s):
                sync.wait_ge(out_ok, after(pair, s))
                sync.dma_start(out[bass.ds(pair * 2 + s, 1)].rearrange("a (b p) d -> p (a b) d", p=P), outN[s][:]).then_inc(out_stored[s], 16)

            def body(pair, first=False, last=False):
                if not last:
                    load(pair + 1, 0, True)
                if not first:
                    store(pair - 1, 0)
                    store(pair - 1, 1)
                if not last:
                    load(pair + 1, 1, True)

            for s in range(2):
                load(0, s, False)
                if s == 0:
                    sync.wait_ge(bse_zero, 1)
                    for dst, src in weight_dmas:
                        sync.dma_start(dst, src).then_inc(w_in, 16)
            pair_loop(sync, lambda p: body(p, first=True), body, lambda p: body(p, last=True))
            for s in range(2):
                store(PAIRS - 1, s)
            for s in range(2):
                sync.wait_ge(out_stored[s], 16 * PAIRS)

        @block.tensor
        def _(pe):
            def split3(o, wh, wl, parts, start, stop):
                nc.tensor.matmul(o, wh, parts[0], start=start, stop=False)
                nc.tensor.matmul(o, wh, parts[1], start=False, stop=False)
                return nc.tensor.matmul(o, wl, parts[0], start=False, stop=stop)

            def first_layer_in(pair, s):
                pe.wait_ge(xT_in[s], loaded(pair))
                for b in range(NB):
                    mm = nc.tensor.matmul(bank(4 + 2 * s)[:, b * D:(b + 1) * D], xT[s][:, b * P:(b + 1) * P], w0T[:],
                                          start=True, stop=True)
                mm.then_inc(y_mm, 1)

            def first_layer_adj(pair, s):
                pe.wait_ge(adjT_in[s], loaded(pair))
                pe.wait_ge(yd_ok, after(pair, s))
                for nb in range(NB):
                    for mb in range(NB):
                        mm = nc.tensor.matmul(bank(5 + 2 * s)[:, nb * D:(nb + 1) * D], adjT[s][:, mb, nb * P:(nb + 1) * P],
                                              yd[s][:, mb, :], start=mb == 0, stop=mb == NB - 1)
                mm.then_inc(l0_mm, 1)

            def transpose_x1(pair, s):
                pe.wait_ge(x1N_ok, after(pair, s))
                for b in range(NB):
                    mm = nc.tensor.transpose(bank(4 + 2 * s)[:, b * P:(b + 1) * P], x1N[s][:, b, :], ident[:])
                mm.then_inc(x1_mm, 1)

            def conv1(pair, s):
                pe.wait_ge(x1h_ok, after(pair, s))
                pe.wait_ge(x1l_ok, after(pair, s))
                split3(bank(5 + 2 * s), w1h[:], w1l[:], (x1h[s][:], x1l[s][:]), True, True).then_inc(c1_mm, 1)

            def embed(pair, s, first):
                if not first:
                    pe.wait_ge((tr_ok, tz_ok)[s], after(pair - 1, 1))
                split3(bank(s), wseh[:], wsel[:], (x1h[s][:], x1l[s][:]), True, True).then_inc(s_mm, 1)

            def message(pair, s, first):
                pe.wait_ge(x1T_ok, after(pair, s))
                if not first:
                    pe.wait_ge((q1_ok, q2_ok)[s], after(pair - 1, 1))
                for b in range(NB):
                    mm = nc.tensor.matmul(bank(2 + s)[:, b * D:(b + 1) * D], x1T[s][:, b * P:(b + 1) * P], wmsgT[:],
                                          start=True, stop=True)
                mm.then_inc(msg_mm, 1)

            def distance(pair, s):
                pe.wait_ge(dR_ok, after(pair, s))
                pe.wait_ge(dL_ok, after(pair, s))
                if s == 0:
                    pe.wait_ge(hh_ok, after(pair, 1))
                    pe.wait_ge(x1l_ok, after(pair, 1))
                else:
                    pe.wait_ge(exp_ok, after(pair, 0))
                for b in range(NB):
                    mm = nc.tensor.matmul(bank(4 + b), dL[s][:, b * P:(b + 1) * P], dR[s][:], start=True, stop=True)
                mm.then_inc(dist_mm, 1)

            def conv2(pair, s):
                pe.wait_ge(hh_ok, after(pair, s))
                pe.wait_ge(hl_ok, after(pair, s))
                for k in range(TAPS):
                    mm = split3(bank(s), w2h[:, k, :], w2l[:, k, :], (hh[s][:, k:k + N], hl[s][:, k:k + N]),
                                k == 0, k == TAPS - 1)
                mm.then_inc(c2_mm, 1)

            def transpose_y1(pair, s, msg_pair):
                pe.wait_ge(y1_ok, after(pair, s))
                if msg_pair is not None:
                    pe.wait_ge(mb_ok, after(msg_pair, s))
                for b in range(NB):
                    mm = nc.tensor.transpose(bank(2 + s)[:, b * P:(b + 1) * P], y1[s][:, b * P:(b + 1) * P], ident[:])
                mm.then_inc(y1_mm, 1)

            def gather(pair, s, first):
                pe.wait_ge(em_ok, after(pair, s))
                pe.wait_ge(msg_ok, after(pair, s))
                pe.wait_ge(mb_ok, after(pair, s))
                if not first:
                    pe.wait_ge(out_ok, after(pair - 1, s))
                for b in range(NB):
                    mm = nc.tensor.matmul(bank(2 + s), msg[s][:, b, :], em[s][:, b, :], start=b == 0, stop=b == NB - 1)
                mm.then_inc(nm_mm, 1)

            def gates(pair, s):
                xs = (x1h[s][:], x1l[s][:])
                xcs = (xch[s][:], xcl[s][:])
                nms = (nmh[s][:], nml[s][:])

                def cols(g):
                    return slice(g * D, (g + 1) * D)
                if s == 0:
                    pe.wait_ge(gc_ok, after(pair, 1))
                    pe.wait_ge(nmh_ok, after(pair, 1))
                    pe.wait_ge(nml_ok, after(pair, 1))
                pe.wait_ge(xch_ok, after(pair, s))
                pe.wait_ge(xcl_ok, after(pair, s))
                pe.wait_ge(nmh_ok, after(pair, s))
                pe.wait_ge(nml_ok, after(pair, s))
                for g, done in ((0, r_mm), (1, z_mm)):
                    if s == 1:
                        pe.wait_ge((tr_ok, tz_ok)[g], after(pair, 0))
                    split3(bank(g), whhh[:, cols(g)], whhl[:, cols(g)], xs, True, False)
                    split3(bank(g), wihh[:, 0, cols(g)], wihl[:, 0, cols(g)], xcs, False, False)
                    split3(bank(g), wihh[:, 1, cols(g)], wihl[:, 1, cols(g)], nms, False, True).then_inc(done, 1)
                if s == 1:
                    pe.wait_ge(q1_ok, after(pair, 0))
                split3(bank(2), whhh[:, cols(2)], whhl[:, cols(2)], xs, True, True).then_inc(hn_mm, 1)
                if s == 1:
                    pe.wait_ge(q2_ok, after(pair, 0))
                split3(bank(3), wihh[:, 0, cols(2)], wihl[:, 0, cols(2)], xcs, True, False)
                split3(bank(3), wihh[:, 1, cols(2)], wihl[:, 1, cols(2)], nms, False, True).then_inc(in_mm, 1)

            def body(pair, first=False, last=False):
                for s in range(2):
                    conv1(pair, s)
                    embed(pair, s, first)
                    message(pair, s, first)
                distance(pair, 0)
                conv2(pair, 0)
                distance(pair, 1)
                if not first:
                    for s in range(2):
                        transpose_y1(pair - 1, s, pair)
                conv2(pair, 1)
                gather(pair, 0, first)
                gather(pair, 1, first)
                if not last:
                    pe.wait_ge(exp_ok, after(pair, 1))
                    for s in range(2):
                        first_layer_in(pair + 1, s)
                    first_layer_adj(pair + 1, 0)
                gates(pair, 0)
                if not last:
                    first_layer_adj(pair + 1, 1)
                    transpose_x1(pair + 1, 0)
                gates(pair, 1)
                if not last:
                    transpose_x1(pair + 1, 1)

            pe.wait_ge(w_in, WEIGHTS_IN)
            for s in range(2):
                first_layer_in(0, s)
            for s in range(2):
                first_layer_adj(0, s)
            pe.wait_ge(w_hi, 5)
            pe.wait_ge(w_lo, 5)
            pe.wait_ge(halo_ok, 4)
            for s in range(2):
                transpose_x1(0, s)
            pair_loop(pe, lambda p: body(p, first=True), body, lambda p: body(p, last=True))
            for s in range(2):
                if s == 0:
                    pe.wait_ge(q1_ok, after(PAIRS - 1, 1))
                else:
                    pe.wait_ge(q2_ok, after(PAIRS - 1, 1))
                transpose_y1(PAIRS - 1, s, None)

        @block.scalar
        def _(act):
            def x1_out(pair, s, first):
                act.wait_ge(x1_mm, after(pair, s))
                if not first:
                    act.wait_ge(e1_ok, after(pair - 1, s))
                    act.wait_ge(e3_ok, after(pair - 1, s))
                    act.wait_ge(in_mm, after(pair - 1, s))
                nc.scalar.activation(x1T[s][:], bank(4 + 2 * s), ACT.Copy).then_inc(x1T_ok, 1)
                nc.scalar.activation(x1h[s][:], bank(4 + 2 * s), ACT.Copy).then_inc(x1h_ok, 1)

            def conv1_out(pair, s, first):
                act.wait_ge(c1_mm, after(pair, s))
                if not first:
                    act.wait_ge(hl_ok, after(pair - 1, s))
                    act.wait_ge(c2_mm, after(pair - 1, s))
                nc.scalar.activation(hT[s][:], bank(5 + 2 * s), ACT.Relu, bias=bn_fac[:, 1:2], scale=bn_fac[:, 0:1]).then_inc(h_ok, 1)
                act.wait_ge(h_ok, after(pair, s))
                nc.scalar.activation(hh[s][:, HALO:HALO + N], hT[s][:], ACT.Copy).then_inc(hh_ok, 1)

            def embed_out(pair, s, first):
                act.wait_ge(s_mm, after(pair, s))
                if not first:
                    act.wait_ge(dL_ok, after(pair - 1, s))
                nc.scalar.activation(sqr[s][:], bank(s), ACT.Square, bias=bse_col[:, 0:1]).then_inc(sqr_ok, 1)
                nc.scalar.activation(slin[s][:], bank(s), ACT.Identity, bias=bse_lin[:, 0:1], scale=coef[:, 1:2]).then_inc(slin_ok, 1)

            def message_out(pair, s):
                act.wait_ge(mb_ok, after(pair, s))
                nc.scalar.activation(msg[s][:], mb_[s][:], ACT.Relu).then_inc(msg_ok, 1)

            def exps(pair, s, first):
                act.wait_ge(dist_mm, after(pair, s))
                if not first:
                    act.wait_ge(nm_mm, after(pair - 1, s))
                nc.scalar.activation(em[s].rearrange("p a b -> p (a b)"), ps[:, 4:8, :].rearrange("p a b -> p (a b)"),
                                     ACT.Exp).then_inc(exp_ok, 1)

            def conv2_out(pair, s, first):
                act.wait_ge(gc_ok, after(pair, s))
                if not first:
                    act.wait_ge(xcl_ok, after(pair - 1, s))
                    act.wait_ge(in_mm, after(pair - 1, s))
                nc.scalar.activation(xch[s][:], gc[s][:], ACT.Relu, bias=bn_fac[:, 3:4]).then_inc(xch_ok, 1)
                nc.scalar.activation(xcT[s][:], gc[s][:], ACT.Relu, bias=bn_fac[:, 3:4]).then_inc(xc_ok, 1)

            def gather_out(pair, s, first):
                act.wait_ge(nm_mm, after(pair, s))
                if not first:
                    act.wait_ge(in_mm, after(pair - 1, s))
                nc.scalar.activation(nmh[s][:], bank(2 + s), ACT.Copy).then_inc(nmh_ok, 1)

            def gates_out(pair, s, first):
                act.wait_ge(r_mm, after(pair, s))
                if not first:
                    act.wait_ge(y1_ok, after(pair - 1, s))
                nc.scalar.activation(tr[s][:], bank(0), ACT.Tanh, bias=gbias[:, 0:1], scale=0.5).then_inc(tr_ok, 1)
                act.wait_ge(z_mm, after(pair, s))
                if not first:
                    act.wait_ge(e2_ok, after(pair - 1, s))
                nc.scalar.activation(tz[s][:], bank(1), ACT.Tanh, bias=gbias[:, 1:2], scale=0.5).then_inc(tz_ok, 1)
                act.wait_ge(q2_ok, after(pair, s))
                nc.scalar.activation(nT[s][:], q2[s][:], ACT.Tanh, bias=bih[:, 2:3]).then_inc(n_ok, 1)

            def body(pair, first=False, last=False):
                for s in range(2):
                    conv1_out(pair, s, first)
                    embed_out(pair, s, first)
                exps(pair, 0, first)
                message_out(pair, 0)
                message_out(pair, 1)
                exps(pair, 1, first)
                conv2_out(pair, 0, first)
                conv2_out(pair, 1, first)
                gather_out(pair, 0, first)
                gather_out(pair, 1, first)
                gates_out(pair, 0, first)
                if not last:
                    x1_out(pair + 1, 0, False)
                gates_out(pair, 1, first)
                if not last:
                    x1_out(pair + 1, 1, False)

            act.wait_ge(w_in, WEIGHTS_IN)
            for dst, src in ((w1h, w1), (w2h, w2), (wihh, wih), (whhh, whh)):
                nc.scalar.activation(dst[:], src, ACT.Copy).then_inc(w_hi, 1)
            act.wait_ge(rep_ok, 2)
            nc.scalar.activation(wseh[:], wse_rep[:], ACT.Copy).then_inc(w_hi, 1)
            act.wait_ge(fold_ok, 1)
            for s in range(2):
                x1_out(0, s, True)
            pair_loop(act, lambda p: body(p, first=True), body, lambda p: body(p, last=True))

        @block.vector
        def _(dve):
            def bcast(v):
                return v[:].unsqueeze(2).to_broadcast([P, NB, D])

            def rows(v):
                return v[:].unsqueeze(1).to_broadcast([P, NB, D])

            def v3(x):
                return x.rearrange("p (b d) -> p b d", b=NB)

            def norm(pair, s, src, st, m, rs, dst, ready, st_ok, mv_ok, rs_ok, rstd_ok, dst_ok, dst_free):
                dve.wait_ge(*ready)
                for b in range(NB):
                    i = nc.vector.bn_stats(st[s][:, b, :], src[:, b, :])
                dve.drain()
                for b in range(NB):
                    i = nc.vector.bn_aggr(m[s][:, b, :], st[s][:, b, :])
                i.then_inc(mv_ok, 1)
                dve.wait_ge(mv_ok, after(pair, s))
                nc.vector.tensor_scalar(rs[s][:], m[s][:, :, 1], EPS, None, ALU.add).then_inc(rs_ok, 1)
                dve.wait_ge(rstd_ok, after(pair, s))
                if dst_free is not None:
                    dve.wait_ge(*dst_free)
                for b in range(NB):
                    i = nc.vector.tensor_scalar(dst[s][:, b, :], src[:, b, :], m[s][:, b, 0:1], rs[s][:, b:b + 1],
                                                ALU.subtract, ALU.mult)
                i.then_inc(dst_ok, 1)

            def degree(pair, s):
                dve.wait_ge(adjN_in[s], loaded(pair))
                nc.vector.tensor_reduce(deg[s][:], adjN[s][:], mybir.AxisListType.X, ALU.add).then_inc(deg_ok, 1)
                dve.wait_ge(deg_ok, after(pair, s))
                nc.vector.tensor_scalar(deg[s][:], deg[s][:], 1.0, None, ALU.add).then_inc(deg1_ok, 1)

            def scale_in(pair, s):
                dve.wait_ge(dinv_ok, after(pair, s))
                dve.wait_ge(y_mm, after(pair, s))
                nc.vector.tensor_tensor(yd[s][:], v3(bank(4 + 2 * s)), bcast(dinv[s]), ALU.mult).then_inc(yd_ok, 1)

            def first_layer_out(pair, s):
                dve.wait_ge(l0_mm, after(pair, s))
                nc.vector.tensor_tensor(z1[s][:], v3(bank(5 + 2 * s)), yd[s][:], ALU.add).then_inc(z1_ok, 1)
                dve.wait_ge(z3_ok, after(pair, s))
                dve.wait_ge(xN_in[s], loaded(pair))
                nc.vector.scalar_tensor_tensor(y0[s][:].rearrange("p b d -> p (b d)"), z3[s][:].rearrange("p b d -> p (b d)"), 0.0, xN[s][:].rearrange("p b d -> p (b d)"), ALU.max, ALU.add).then_inc(y0_ok, 1)
                norm(pair, s, y0[s], stats, mv, rstd, x1N, (y0_ok, after(pair, s)), st_ok, mv_ok, rs_ok, rstd_ok, x1N_ok, None)

            def x1_lo(pair, s, first):
                dve.wait_ge(x1h_ok, after(pair, s))
                dve.wait_ge(x1T_ok, after(pair, s))
                nc.vector.tensor_tensor(x1l[s][:], x1T[s][:], x1h[s][:].bitcast(FP32), ALU.subtract).then_inc(x1l_ok, 1)

            def h_lo(pair, s):
                dve.wait_ge(hh_ok, after(pair, s))
                nc.vector.tensor_tensor(hl[s][:, HALO:HALO + N], hT[s][:], hh[s][:, HALO:HALO + N].bitcast(FP32), ALU.subtract).then_inc(hl_ok, 1)

            def dist_operands(pair, s):
                dve.wait_ge(sqr_ok, after(pair, s))
                dve.wait_ge(slin_ok, after(pair, s))
                nc.vector.scalar_tensor_tensor(su[s][:], sqr[s][:], coef[:, 0:1], slin[s][:], ALU.mult, ALU.add).then_inc(su_ok, 1)
                dve.wait_ge(su_ok, after(pair, s))
                nc.vector.tensor_copy(suh[s][:], su[s][:]).then_inc(suh_ok, 1)
                nc.vector.tensor_scalar(suR[s][:], su[s][:], coef[:, 3:4], coef[:, 4:5], ALU.mult, ALU.add).then_inc(suR_ok, 1)
                nc.vector.tensor_scalar(suL[s][:], su[s][:], coef[:, 6:7], coef[:, 7:8], ALU.mult, ALU.add).then_inc(suL_ok, 1)
                dve.wait_ge(suh_ok, after(pair, s))
                dve.wait_ge(suR_ok, after(pair, s))
                nc.vector.scalar_tensor_tensor(dR[s][:], suh[s][:].bitcast(FP32), coef[:, 2:3], suR[s][:], ALU.mult, ALU.add).then_inc(dR_ok, 1)
                dve.wait_ge(suL_ok, after(pair, s))
                nc.vector.scalar_tensor_tensor(dL[s][:], suh[s][:].bitcast(FP32), coef[:, 5:6], suL[s][:], ALU.mult, ALU.add).then_inc(dL_ok, 1)

            def message_out(pair, s, first):
                dve.wait_ge(msg_mm, after(pair, s))
                if not first:
                    dve.wait_ge(nm_mm, after(pair - 1, s))
                nc.vector.tensor_tensor(mb_[s][:], v3(bank(2 + s)), rows(bmsg_rep), ALU.add).then_inc(mb_ok, 1)

            def mask(pair, s):
                dve.wait_ge(exp_ok, after(pair, s))
                nc.vector.tensor_tensor(em[s], em[s], adjT[s][:], ALU.mult).then_inc(em_ok, 1)

            def conv2_out(pair, s):
                dve.wait_ge(c2_mm, after(pair, s))
                nc.vector.scalar_tensor_tensor(gc[s][:], bank(s), bn_fac[:, 2:3], x1T[s][:], ALU.mult, ALU.add).then_inc(gc_ok, 1)

            def xc_lo(pair, s):
                dve.wait_ge(xc_ok, after(pair, s))
                dve.wait_ge(xch_ok, after(pair, s))
                nc.vector.tensor_tensor(xcl[s][:], xcT[s][:], xch[s][:].bitcast(FP32), ALU.subtract).then_inc(xcl_ok, 1)

            def nm_lo(pair, s):
                dve.wait_ge(nmh_ok, after(pair, s))
                nc.vector.tensor_tensor(nml[s][:], bank(2 + s), nmh[s][:].bitcast(FP32), ALU.subtract).then_inc(nml_ok, 1)

            def gates_out(pair, s, first):
                dve.wait_ge(tr_ok, after(pair, s))
                nc.vector.tensor_scalar(tr1[s][:], tr[s][:], 1.0, 0.5, ALU.add, ALU.mult).then_inc(tr1_ok, 1)
                dve.wait_ge(tr1_ok, after(pair, s))
                dve.wait_ge(hn_mm, after(pair, s))
                nc.vector.scalar_tensor_tensor(q1[s][:], bank(2), bhh[:, 2:3], tr1[s][:], ALU.add, ALU.mult).then_inc(q1_ok, 1)
                dve.wait_ge(q1_ok, after(pair, s))
                dve.wait_ge(in_mm, after(pair, s))
                nc.vector.tensor_tensor(q2[s][:], bank(3), q1[s][:], ALU.add).then_inc(q2_ok, 1)
                dve.wait_ge(n_ok, after(pair, s))
                if not first:
                    dve.wait_ge(y1_mm, after(pair - 1, s))
                nc.vector.tensor_tensor(e1[s][:], x1T[s][:], nT[s][:], ALU.subtract).then_inc(e1_ok, 1)
                dve.wait_ge(e1_ok, after(pair, s))
                nc.vector.scalar_tensor_tensor(e2[s][:], tz[s][:], 1.0, e1[s][:], ALU.add, ALU.mult).then_inc(e2_ok, 1)
                dve.wait_ge(e2_ok, after(pair, s))
                dve.wait_ge(e3_ok, after(pair, s))
                nc.vector.scalar_tensor_tensor(y1[s][:], e2[s][:], 0.5, e3[s][:], ALU.mult, ALU.add).then_inc(y1_ok, 1)

            def second_norm(pair, s, stored):
                free = (out_stored[s], 16 * stored) if stored is not None else None
                norm(pair, s, v3(bank(2 + s)), stats1, mv1, rstd1, outN, (y1_mm, after(pair, s)), st1_ok, mv1_ok, rs1_ok,
                     rstd1_ok, out_ok, free)

            def body(pair, first=False, last=False, stored=None):
                for s in range(2):
                    h_lo(pair, s)
                    dist_operands(pair, s)
                    message_out(pair, s, first)
                mask(pair, 0)
                conv2_out(pair, 0)
                xc_lo(pair, 0)
                mask(pair, 1)
                if not first:
                    for s in range(2):
                        second_norm(pair - 1, s, stored)
                conv2_out(pair, 1)
                xc_lo(pair, 1)
                nm_lo(pair, 0)
                nm_lo(pair, 1)
                if not last:
                    for s in range(2):
                        degree(pair + 1, s)
                    for s in range(2):
                        scale_in(pair + 1, s)
                    first_layer_out(pair + 1, 0)
                gates_out(pair, 0, first)
                if not last:
                    first_layer_out(pair + 1, 1)
                    x1_lo(pair + 1, 0, False)
                gates_out(pair, 1, first)
                if not last:
                    x1_lo(pair + 1, 1, False)

            nc.vector.memset(wse_rep[:], 0.0).then_inc(rep_ok, 1)
            dve.wait_ge(w_in, WEIGHTS_IN)
            dve.wait_ge(rep_ok, 1)
            nc.vector.tensor_copy(wse_rep[:, 0:DIST_ROWS].rearrange("p (a b) -> p a b", b=SE),
                                  wseT[:].unsqueeze(1).to_broadcast([P, DIST_ROWS // SE, SE])).then_inc(rep_ok, 1)
            bn4 = bn[:].rearrange("p (l k) -> p k l", l=2)
            fac = bn_fac[:].rearrange("p (l k) -> p k l", l=2)
            nc.vector.tensor_scalar(bn_tmp[:, 0:2], bn4[:, 3, :], EPS, None, ALU.add).then_inc(fold_var, 1)
            nc.vector.tensor_tensor(gbias2[:, 0:2], bih[:, 0:2], bhh[:, 0:2], ALU.add).then_inc(fold_step, 1)
            nc.vector.tensor_tensor(bse_lin[:], bse_col[:], coef[:, 1:2], ALU.mult).then_inc(fold_step, 1)
            dve.wait_ge(fold_step, 2)
            dve.wait_ge(fold_pow, 1)
            nc.vector.tensor_tensor(fac[:, 0, :], bn4[:, 0, :], bn_tmp[:, 0:2], ALU.mult).then_inc(fold_step, 1)
            nc.vector.tensor_scalar(gbias[:, 0:2], gbias2[:, 0:2], 0.5, None, ALU.mult).then_inc(fold_step, 1)
            dve.wait_ge(fold_step, 4)
            nc.vector.tensor_tensor(bn_tmp[:, 2:4], bn4[:, 2, :], fac[:, 0, :], ALU.mult).then_inc(fold_step, 1)
            dve.wait_ge(fold_step, 5)
            nc.vector.tensor_tensor(fac[:, 1, :], bn4[:, 1, :], bn_tmp[:, 2:4], ALU.subtract).then_inc(fold_ok, 1)
            for i, (lo, whole, hi) in enumerate(((w1l, w1, w1h), (w2l, w2, w2h), (wihl, wih, wihh), (whhl, whh, whhh),
                                                 (wsel, wse_rep[:], wseh))):
                dve.wait_ge(w_hi, i + 1)
                nc.vector.tensor_tensor(lo[:], whole, hi[:].bitcast(FP32), ALU.subtract).then_inc(w_lo, 1)
            for s in range(2):
                degree(0, s)
            for s in range(2):
                scale_in(0, s)
            for s in range(2):
                first_layer_out(0, s)
            for s in range(2):
                x1_lo(0, s, True)
            body(0, first=True)
            body(1, stored=None)
            with dve.Fori(2, PAIRS - 1) as pair:
                body(pair, stored=pair - 1)
            body(PAIRS - 1, last=True, stored=PAIRS - 2)
            for s in range(2):
                second_norm(PAIRS - 1, s, PAIRS - 1)

        @block.gpsimd
        def _(pool):
            def rsqrt(tile, ready, done):
                pool.wait_ge(*ready)
                nc.gpsimd.tensor_tensor(tile, tile, neg_half[:, 0:tile.shape[1]], ALU.pow).then_inc(done, 1)

            def degrees(pair, s, first):
                pool.wait_ge(deg1_ok, after(pair, s))
                nc.gpsimd.tensor_tensor(dinv[s][:], deg[s][:], neg_half[:], ALU.pow).then_inc(dinv_ok, 1)

            def first_layer_out(pair, s):
                pool.wait_ge(z1_ok, after(pair, s))
                nc.gpsimd.tensor_tensor(z2[s][:], z1[s][:], dinv[s][:].unsqueeze(2).to_broadcast([P, NB, D]), ALU.mult).then_inc(z2_ok, 1)
                pool.wait_ge(z2_ok, after(pair, s))
                nc.gpsimd.tensor_tensor(z3[s][:], z2[s][:], b0_rep[:].unsqueeze(1).to_broadcast([P, NB, D]), ALU.add).then_inc(z3_ok, 1)
                rsqrt(rstd[s][:], (rs_ok, after(pair, s)), rstd_ok)

            def gates_out(pair, s, first):
                pool.wait_ge(n_ok, after(pair, s))
                nc.gpsimd.tensor_tensor(e3[s][:], x1T[s][:], nT[s][:], ALU.add).then_inc(e3_ok, 1)

            def body(pair, first=False, last=False):
                if not first:
                    for s in range(2):
                        rsqrt(rstd1[s][:], (rs1_ok, after(pair - 1, s)), rstd1_ok)
                if not last:
                    for s in range(2):
                        degrees(pair + 1, s, False)
                    first_layer_out(pair + 1, 0)
                gates_out(pair, 0, first)
                if not last:
                    first_layer_out(pair + 1, 1)
                gates_out(pair, 1, first)

            nc.gpsimd.memset(bse_col[:], 0.0).then_inc(bse_zero, 1)
            nc.gpsimd.memset(neg_half[:], -0.5).then_inc(half_ok, 1)
            for tile in hh + hl:
                halos = tile[:].bitcast(FP32)
                nc.gpsimd.memset(halos[:, 0:HALO], 0.0)
                nc.gpsimd.memset(halos[:, HALO + N:N + 2 * HALO], 0.0).then_inc(halo_ok, 1)
            pool.wait_ge(half_ok, 1)
            rsqrt(bn_tmp[:, 0:2], (fold_var, 1), fold_pow)
            for s in range(2):
                degrees(0, s, True)
            for s in range(2):
                first_layer_out(0, s)
            pair_loop(pool, lambda p: body(p, first=True), body, lambda p: body(p, last=True))
            for s in range(2):
                rsqrt(rstd1[s][:], (rs1_ok, after(PAIRS - 1, s)), rstd1_ok)


def kernel(**inputs):
    import numpy as np
    from concourse import bacc
    from concourse.bass_utils import run_bass_kernel_spmd

    a = {k: np.asarray(v) for k, v in inputs.items()}
    L = {k[len("L1_gnn_"):]: v for k, v in a.items() if k.startswith("L1_gnn_")}
    arrays = {
        "adjN": a["adj"], "adjT": a["adj"].transpose(0, 2, 1), "xN": a["x"], "xT": a["x"].transpose(0, 2, 1),
        "w0T": a["L0_gnn_W"].T, "b0": a["L0_gnn_b"], "wmsgT": L["w_msg"].T, "bmsg": L["b_msg"],
        "wseT": L["w_se"].T, "bse": L["b_se"], "w1T": L["conv1_w"][:, :, 0].T, "w2T": L["conv2_w"].transpose(1, 2, 0),
        "wihT": L["w_ih"].T, "whhT": L["w_hh"].T, "bih": L["b_ih"].reshape(3, D).T, "bhh": L["b_hh"].reshape(3, D).T,
        "bn": np.stack([L[f"bn{i}_{k}"] for i in (1, 2) for k in "gbmv"], axis=1),
        "ident": np.eye(P, dtype=np.float32), "coef": distance_factors(),
    }
    arrays = {f"in_{k}": np.ascontiguousarray(v) for k, v in arrays.items()}
    nc = bacc.Bacc("TRN2", target_bir_lowering=False, num_devices=1)
    t = {k[3:]: nc.dram_tensor(k, v.shape, mybir.dt.from_np(v.dtype), kind="ExternalInput").ap() for k, v in arrays.items()}
    out = nc.dram_tensor("out", (G, N, D), FP32, kind="ExternalOutput").ap()
    gnn_kernel(nc, t, out)
    r = run_bass_kernel_spmd(nc, [arrays], core_ids=[0])
    return r.results[0]["out"]
```

```python
from contextlib import ExitStack

import concourse.bass as bass
from concourse import mybir

FP32 = mybir.dt.float32
FP32R = mybir.dt.float32r
ACT = mybir.ActivationFunctionType
ALU = mybir.AluOpType

G, N, D, TAPS, SE = 16, 512, 128, 17, 3
P = 128
NB = N // P
PAIRS = G // 2
HALO = TAPS // 2
SPLIT_0, SPLIT_1 = 11, 8
EPS = 1e-5
DIST_ROWS = 8 * SE


def distance_factors():
    import numpy as np
    hi, lo, minus = (1, 0, 0), (-1, 1, 0), (0, 0, -1)
    twice = lambda f: tuple(2 * x for x in f)
    kinds = [(0, hi, twice(hi)), (0, lo, twice(hi)), (0, hi, twice(lo)), (0, lo, twice(lo)),
             (1, hi, minus), (1, lo, minus), (1, minus, hi), (1, minus, lo)]
    f = np.zeros((P, 8), np.float32)
    for i, (square, moving, stationary) in enumerate(kinds):
        f[SE * i:SE * (i + 1)] = (square, 1 - square) + moving + stationary
    return f


def after(pair, slot):
    return pair * 2 + (slot + 1)


def loaded(pair):
    return (pair + 1) * 16


def gnn_kernel(nc, t, out):
    ctx = ExitStack()
    with ctx:
        def sb(name, shape, dt=FP32):
            return ctx.enter_context(nc.sbuf_tensor(name, shape, dt))

        def sem(name):
            return ctx.enter_context(nc.semaphore(name))

        ident = sb("ident", [P, P])
        coef = sb("coef", [P, 8])
        w0T = sb("w0T", [P, D])
        b0_rep = sb("b0_rep", [P, D])
        bmsg_rep = sb("bmsg_rep", [P, D])
        wmsgT = sb("wmsgT", [P, D])
        wseT = sb("wseT", [P, SE])
        wse_rep = sb("wse_rep", [P, P])
        bse_col = sb("bse_col", [P, 1])
        bse_lin = sb("bse_lin", [P, 1])
        w1h, w1l = sb("w1h", [P, D], FP32R), sb("w1l", [P, D], FP32R)
        w2h, w2l = sb("w2h", [P, TAPS, D], FP32R), sb("w2l", [P, TAPS, D], FP32R)
        wihh, wihl = sb("wihh", [P, 2, 3 * D], FP32R), sb("wihl", [P, 2, 3 * D], FP32R)
        whhh, whhl = sb("whhh", [P, 3 * D], FP32R), sb("whhl", [P, 3 * D], FP32R)
        wseh, wsel = sb("wseh", [P, P], FP32R), sb("wsel", [P, P], FP32R)
        bn = sb("bn", [P, 8])
        bn_fac = sb("bn_fac", [P, 4])
        bn_tmp = sb("bn_tmp", [P, 4])
        bih, bhh = sb("bih", [P, 3]), sb("bhh", [P, 3])
        gbias2 = sb("gbias2", [P, 2])
        neg_half = sb("neg_half", [P, NB])
        gbias = sb("gbias", [P, 2])

        def two(name, shape, dt=FP32):
            return [sb(f"{name}{s}", shape, dt) for s in range(2)]

        adjT = two("adjT", [P, NB, N])
        adjN = two("adjN", [P, NB, N])
        xT = two("xT", [P, N])
        xN = two("xN", [P, NB, D])
        deg = two("deg", [P, NB])
        dinv = two("dinv", [P, NB])
        yd = two("yd", [P, NB, D])
        z1 = z2 = z3 = y0 = x1N = two("x1N", [P, NB, D])
        stats = two("stats", [P, NB, 6])
        mv = two("mv", [P, NB, 2])
        rstd = two("rstd", [P, NB])
        x1T = two("x1T", [P, N])
        x1h, x1l = two("x1h", [P, N], FP32R), two("x1l", [P, N], FP32R)
        hT = two("hT", [P, N])
        hh = two("hh", [P, N + 2 * HALO], FP32R)
        hl = two("hl", [P, N + 2 * HALO], FP32R)
        sqr = su = suL = two("suL", [P, N])
        slin = suR = two("suR", [P, N])
        suh = two("suh", [P, N], FP32R)
        dR, dL = two("dR", [P, N], FP32R), two("dL", [P, N], FP32R)
        mb_ = msg = two("msg", [P, NB, D])
        em_both = sb("em", [P, 2, NB, N])
        em = [em_both[:, s] for s in range(2)]
        gc = xcT = two("xcT", [P, N])
        xch, xcl = two("xch", [P, N], FP32R), two("xcl", [P, N], FP32R)
        nmh, nml = two("nmh", [P, N], FP32R), two("nml", [P, N], FP32R)
        tr = tr1 = q1 = q2 = nT = two("nT", [P, N])
        tz = two("tz", [P, N])
        e1 = e2 = y1 = two("y1", [P, N])
        e3 = two("e3", [P, N])
        stats1 = two("stats1", [P, NB, 6])
        mv1 = two("mv1", [P, NB, 2])
        rstd1 = two("rstd1", [P, NB])
        outN = two("outN", [P, NB, D])

        at, parts = 0, []
        for width in (TAPS * D, 2 * 3 * D, 3 * D, D):
            parts.append(em_both[:].rearrange("p s b n -> p (s b n)")[:, at:at + width])
            at += width
        w2, wih = parts[0].rearrange("p (k o) -> p k o", k=TAPS), parts[1].rearrange("p (k o) -> p k o", k=2)
        whh, w1 = parts[2], parts[3]

        ps = ctx.enter_context(nc.psum_tensor("ps", [P, 8, N], FP32))

        X1_BANK = (4, 1)

        def bank(i):
            return ps[:, i, :]

        w_in = sem("w_in")
        w_hi, w_lo = sem("w_hi"), sem("w_lo")
        rep_ok, fold_ok, fold_step = sem("rep_ok"), sem("fold_ok"), sem("fold_step")
        half_ok, fold_var, fold_pow = sem("half_ok"), sem("fold_var"), sem("fold_pow")
        halo_ok, bse_zero = sem("halo_ok"), sem("bse_zero")
        adjT_in = [sem(f"adjT_in{s}") for s in range(2)]
        adjN_in = [sem(f"adjN_in{s}") for s in range(2)]
        xT_in = [sem(f"xT_in{s}") for s in range(2)]
        xN_in = [sem(f"xN_in{s}") for s in range(2)]
        out_stored = [sem(f"out_stored{s}") for s in range(2)]
        (deg_ok, deg1_ok, dinv_ok, y_mm, yd_ok, l0_mm, z1_ok, z2_ok, z3_ok, y0_ok, st_ok, mv_ok, rs_ok, rstd_ok, x1N_ok,
         x1_mm, x1T_ok, x1h_ok, x1l_ok, c1_mm, h_ok, hh_ok, hl_ok, s_mm, sqr_ok, slin_ok, su_ok, suh_ok, suR_ok,
         suL_ok, dR_ok, dL_ok, msg_mm, mb_ok, msg_ok, dist_mm, exp_ok, em_ok, c2_mm, gc_ok, xc_ok, xch_ok, xcl_ok,
         nm_mm, nmh_ok, nml_ok, r_mm, z_mm, hn_mm, in_mm, tr_ok, tz_ok, tr1_ok, q1_ok, q2_ok, n_ok, e1_ok, e2_ok,
         e3_ok, y1_ok, y1_mm, st1_ok, mv1_ok, rs1_ok, rstd1_ok, out_ok) = (sem(x) for x in (
            "deg_ok deg1_ok dinv_ok y_mm yd_ok l0_mm z1_ok z2_ok z3_ok y0_ok st_ok mv_ok rs_ok rstd_ok x1N_ok "
            "x1_mm x1T_ok x1h_ok x1l_ok c1_mm h_ok hh_ok hl_ok s_mm sqr_ok slin_ok su_ok suh_ok suR_ok "
            "suL_ok dR_ok dL_ok msg_mm mb_ok msg_ok dist_mm exp_ok em_ok c2_mm gc_ok xc_ok xch_ok xcl_ok "
            "nm_mm nmh_ok nml_ok r_mm z_mm hn_mm in_mm tr_ok tz_ok tr1_ok q1_ok q2_ok n_ok e1_ok e2_ok "
            "e3_ok y1_ok y1_mm st1_ok mv1_ok rs1_ok rstd1_ok out_ok").split())

        weight_dmas = [
            (ident[:], t["ident"]), (coef[:], t["coef"]), (w0T[:], t["w0T"]), (wmsgT[:], t["wmsgT"]),
            (wseT[:], t["wseT"]), (w1, t["w1T"]), (w2, t["w2T"]),
            (wih[:, 0, :], t["wihT"][0:P, :]), (wih[:, 1, :], t["wihT"][P:2 * P, :]), (whh, t["whhT"]),
            (b0_rep[:], t["b0"].partition_broadcast(P)), (bmsg_rep[:], t["bmsg"].partition_broadcast(P)),
            (bih[:], t["bih"]), (bhh[:], t["bhh"]),
        ]
        weight_dmas.append((bn[:], t["bn"]))
        for i in range(DIST_ROWS // SE):
            weight_dmas.append((bse_col[SE * i:SE * (i + 1), :], t["bse"].rearrange("(p a) -> p a", a=1)))
        WEIGHTS_IN = 16 * len(weight_dmas)

        block = ctx.enter_context(nc.Block())

        def pair_loop(eng, first, body, last):
            first(0)
            with eng.Fori(1, PAIRS - 1) as pair:
                body(pair)
            last(PAIRS - 1)

        @block.sync
        def _(sync):
            def load_nodes(pair, s, reuse):
                g = bass.ds(pair * 2 + s, 1)
                if reuse:
                    sync.wait_ge(deg_ok, after(pair - 1, s))
                    sync.wait_ge(y_mm, after(pair - 1, s))
                sync.dma_start(xT[s][:], t["xT"][g].rearrange("a p n -> p (a n)")).then_inc(xT_in[s], 16)
                sync.dma_start(adjN[s][:], t["adjN"][g].rearrange("a (b p) n -> p (a b) n", p=P)).then_inc(adjN_in[s], 16)
                if reuse:
                    sync.wait_ge(y0_ok, after(pair - 1, s))
                sync.dma_start(xN[s][:], t["xN"][g].rearrange("a (b p) n -> p (a b) n", p=P)).then_inc(xN_in[s], 16)

            def load_edges(pair, s, reuse):
                if reuse:
                    sync.wait_ge(em_ok, after(pair - 1, s))
                sync.dma_start(adjT[s][:], t["adjT"][bass.ds(pair * 2 + s, 1)].rearrange("a (b p) n -> p (a b) n", p=P)).then_inc(adjT_in[s], 16)

            def store(pair, s):
                sync.wait_ge(out_ok, after(pair, s))
                sync.dma_start(out[bass.ds(pair * 2 + s, 1)].rearrange("a (b p) d -> p (a b) d", p=P), outN[s][:]).then_inc(out_stored[s], 16)

            def body(pair, first=False, last=False):
                if not last:
                    load_nodes(pair + 1, 0, True)
                    load_nodes(pair + 1, 1, True)
                    load_edges(pair + 1, 0, True)
                if not first:
                    store(pair - 1, 0)
                    store(pair - 1, 1)
                if not last:
                    load_edges(pair + 1, 1, True)

            for s in range(2):
                load_nodes(0, s, False)
                load_edges(0, s, False)
                if s == 0:
                    sync.wait_ge(bse_zero, 1)
                    for dst, src in weight_dmas:
                        sync.dma_start(dst, src).then_inc(w_in, 16)
            pair_loop(sync, lambda p: body(p, first=True), body, lambda p: body(p, last=True))
            for s in range(2):
                store(PAIRS - 1, s)
            for s in range(2):
                sync.wait_ge(out_stored[s], 16 * PAIRS)

        @block.tensor
        def _(pe):
            def split3(o, wh, wl, parts, start, stop):
                nc.tensor.matmul(o, wh, parts[0], start=start, stop=False)
                nc.tensor.matmul(o, wh, parts[1], start=False, stop=False)
                return nc.tensor.matmul(o, wl, parts[0], start=False, stop=stop)

            def first_layer_in(pair, s):
                pe.wait_ge(xT_in[s], loaded(pair))
                for b in range(NB):
                    mm = nc.tensor.matmul(bank(4 + 2 * s)[:, b * D:(b + 1) * D], xT[s][:, b * P:(b + 1) * P], w0T[:],
                                          start=True, stop=True)
                mm.then_inc(y_mm, 1)

            def first_layer_adj(pair, s):
                pe.wait_ge(adjT_in[s], loaded(pair))
                pe.wait_ge(yd_ok, after(pair, s))
                for nb in range(NB):
                    for mb in range(NB):
                        mm = nc.tensor.matmul(bank(5 + 2 * s)[:, nb * D:(nb + 1) * D], adjT[s][:, mb, nb * P:(nb + 1) * P],
                                              yd[s][:, mb, :], start=mb == 0, stop=mb == NB - 1)
                mm.then_inc(l0_mm, 1)

            def transpose_x1(pair, s, first):
                pe.wait_ge(x1N_ok, after(pair, s))
                if s == 1 and not first:
                    pe.wait_ge(tz_ok, after(pair - 1, 1))
                for b in range(NB):
                    mm = nc.tensor.transpose(bank(X1_BANK[s])[:, b * P:(b + 1) * P], x1N[s][:, b, :], ident[:])
                mm.then_inc(x1_mm, 1)

            def conv1(pair, s):
                pe.wait_ge(x1h_ok, after(pair, s))
                pe.wait_ge(x1l_ok, after(pair, s))
                if s == 1:
                    pe.wait_ge(exp_ok, after(pair, 0))
                split3(bank(5 + 2 * s), w1h[:], w1l[:], (x1h[s][:], x1l[s][:]), True, True).then_inc(c1_mm, 1)

            def embed(pair, s, first):
                if not first and s == 0:
                    pe.wait_ge(tr_ok, after(pair - 1, 1))
                split3(bank(s), wseh[:], wsel[:], (x1h[s][:], x1l[s][:]), True, True).then_inc(s_mm, 1)

            def message(pair, s, first):
                pe.wait_ge(x1T_ok, after(pair, s))
                if not first:
                    pe.wait_ge((q1_ok, q2_ok)[s], after(pair - 1, 1))
                for b in range(NB):
                    mm = nc.tensor.matmul(bank(2 + s)[:, b * D:(b + 1) * D], x1T[s][:, b * P:(b + 1) * P], wmsgT[:],
                                          start=True, stop=True)
                mm.then_inc(msg_mm, 1)

            def distance(pair, s):
                pe.wait_ge(dR_ok, after(pair, s))
                pe.wait_ge(dL_ok, after(pair, s))
                pe.wait_ge(hh_ok, after(pair, s))
                for b in range(NB):
                    mm = nc.tensor.matmul(bank(4 + b), dL[s][:, b * P:(b + 1) * P], dR[s][:], start=True, stop=True)
                mm.then_inc(dist_mm, 1)

            def conv2(pair, s, taps):
                if taps[0] == 0:
                    pe.wait_ge(hh_ok, after(pair, s))
                    pe.wait_ge(hl_ok, after(pair, s))
                    pe.wait_ge(sqr_ok, after(pair, s))
                    pe.wait_ge(slin_ok, after(pair, s))
                for k in taps:
                    mm = split3(bank(s), w2h[:, k, :], w2l[:, k, :], (hh[s][:, k:k + N], hl[s][:, k:k + N]),
                                k == 0, k == TAPS - 1)
                if taps[-1] == TAPS - 1:
                    mm.then_inc(c2_mm, 1)

            def transpose_y1(pair, s, msg_pair):
                pe.wait_ge(y1_ok, after(pair, s))
                if msg_pair is not None:
                    pe.wait_ge(mb_ok, after(msg_pair, s))
                for b in range(NB):
                    mm = nc.tensor.transpose(bank(2 + s)[:, b * P:(b + 1) * P], y1[s][:, b * P:(b + 1) * P], ident[:])
                mm.then_inc(y1_mm, 1)

            def gather(pair, s, first):
                pe.wait_ge(em_ok, after(pair, s))
                pe.wait_ge(msg_ok, after(pair, s))
                pe.wait_ge(mb_ok, after(pair, s))
                if not first:
                    pe.wait_ge(out_ok, after(pair - 1, s))
                for b in range(NB):
                    mm = nc.tensor.matmul(bank(2 + s), msg[s][:, b, :], em[s][:, b, :], start=b == 0, stop=b == NB - 1)
                mm.then_inc(nm_mm, 1)

            def gates(pair, s):
                xs = (x1h[s][:], x1l[s][:])
                xcs = (xch[s][:], xcl[s][:])
                nms = (nmh[s][:], nml[s][:])

                def cols(g):
                    return slice(g * D, (g + 1) * D)
                if s == 0:
                    pe.wait_ge(gc_ok, after(pair, 1))
                    pe.wait_ge(nmh_ok, after(pair, 1))
                    pe.wait_ge(nml_ok, after(pair, 1))
                pe.wait_ge(xch_ok, after(pair, s))
                pe.wait_ge(xcl_ok, after(pair, s))
                pe.wait_ge(nmh_ok, after(pair, s))
                pe.wait_ge(nml_ok, after(pair, s))
                for g, done in ((0, r_mm), (1, z_mm)):
                    if s == 1:
                        pe.wait_ge((tr_ok, tz_ok)[g], after(pair, 0))
                    split3(bank(g), whhh[:, cols(g)], whhl[:, cols(g)], xs, True, False)
                    split3(bank(g), wihh[:, 0, cols(g)], wihl[:, 0, cols(g)], xcs, False, False)
                    split3(bank(g), wihh[:, 1, cols(g)], wihl[:, 1, cols(g)], nms, False, True).then_inc(done, 1)
                if s == 1:
                    pe.wait_ge(q1_ok, after(pair, 0))
                split3(bank(2), whhh[:, cols(2)], whhl[:, cols(2)], xs, True, True).then_inc(hn_mm, 1)
                if s == 1:
                    pe.wait_ge(q2_ok, after(pair, 0))
                split3(bank(3), wihh[:, 0, cols(2)], wihl[:, 0, cols(2)], xcs, True, False)
                split3(bank(3), wihh[:, 1, cols(2)], wihl[:, 1, cols(2)], nms, False, True).then_inc(in_mm, 1)

            def body(pair, first=False, last=False):
                conv1(pair, 0)
                embed(pair, 0, first)
                message(pair, 0, first)
                conv2(pair, 0, range(0, SPLIT_0))
                transpose_x1(pair, 1, first)
                distance(pair, 0)
                conv2(pair, 0, range(SPLIT_0, TAPS))
                conv1(pair, 1)
                embed(pair, 1, first)
                message(pair, 1, first)
                conv2(pair, 1, range(0, SPLIT_1))
                distance(pair, 1)
                if not first:
                    for s in range(2):
                        transpose_y1(pair - 1, s, pair)
                conv2(pair, 1, range(SPLIT_1, TAPS))
                if not last:
                    pe.wait_ge(exp_ok, after(pair, 1))
                    for s in range(2):
                        first_layer_in(pair + 1, s)
                gather(pair, 0, first)
                gather(pair, 1, first)
                if not last:
                    first_layer_adj(pair + 1, 0)
                gates(pair, 0)
                gates(pair, 1)
                if not last:
                    transpose_x1(pair + 1, 0, False)
                    first_layer_adj(pair + 1, 1)

            pe.wait_ge(w_in, WEIGHTS_IN)
            for s in range(2):
                first_layer_in(0, s)
            first_layer_adj(0, 0)
            first_layer_adj(0, 1)
            transpose_x1(0, 0, True)
            pe.wait_ge(w_hi, 5)
            pe.wait_ge(w_lo, 5)
            pe.wait_ge(halo_ok, 4)
            pair_loop(pe, lambda p: body(p, first=True), body, lambda p: body(p, last=True))
            for s in range(2):
                pe.wait_ge((q1_ok, q2_ok)[s], after(PAIRS - 1, 1))
                transpose_y1(PAIRS - 1, s, None)

        @block.scalar
        def _(act):
            def x1_out(pair, s, first):
                act.wait_ge(x1_mm, after(pair, s))
                if not first:
                    act.wait_ge(e1_ok, after(pair - 1, s))
                    act.wait_ge(e3_ok, after(pair - 1, s))
                    act.wait_ge(in_mm, after(pair - 1, s))
                nc.scalar.activation(x1T[s][:], bank(X1_BANK[s]), ACT.Copy).then_inc(x1T_ok, 1)
                nc.scalar.activation(x1h[s][:], bank(X1_BANK[s]), ACT.Copy).then_inc(x1h_ok, 1)

            def conv1_out(pair, s, first):
                act.wait_ge(c1_mm, after(pair, s))
                if not first:
                    act.wait_ge(hl_ok, after(pair - 1, s))
                    act.wait_ge(c2_mm, after(pair - 1, s))
                nc.scalar.activation(hT[s][:], bank(5 + 2 * s), ACT.Relu, bias=bn_fac[:, 1:2], scale=bn_fac[:, 0:1]).then_inc(h_ok, 1)
                nc.scalar.activation(hh[s][:, HALO:HALO + N], bank(5 + 2 * s), ACT.Relu, bias=bn_fac[:, 1:2], scale=bn_fac[:, 0:1]).then_inc(hh_ok, 1)

            def embed_out(pair, s, first):
                act.wait_ge(s_mm, after(pair, s))
                if not first:
                    act.wait_ge(dL_ok, after(pair - 1, s))
                nc.scalar.activation(sqr[s][:], bank(s), ACT.Square, bias=bse_col[:, 0:1]).then_inc(sqr_ok, 1)
                nc.scalar.activation(slin[s][:], bank(s), ACT.Identity, bias=bse_lin[:, 0:1], scale=coef[:, 1:2]).then_inc(slin_ok, 1)

            def message_out(pair, s):
                act.wait_ge(mb_ok, after(pair, s))
                nc.scalar.activation(msg[s][:], mb_[s][:], ACT.Relu).then_inc(msg_ok, 1)

            def exps(pair, s, first):
                act.wait_ge(dist_mm, after(pair, s))
                if not first:
                    act.wait_ge(nm_mm, after(pair - 1, s))
                nc.scalar.activation(em[s].rearrange("p a b -> p (a b)"), ps[:, 4:8, :].rearrange("p a b -> p (a b)"),
                                     ACT.Exp).then_inc(exp_ok, 1)

            def conv2_out(pair, s, first):
                act.wait_ge(gc_ok, after(pair, s))
                if not first:
                    act.wait_ge(xcl_ok, after(pair - 1, s))
                    act.wait_ge(in_mm, after(pair - 1, s))
                nc.scalar.activation(xch[s][:], gc[s][:], ACT.Relu, bias=bn_fac[:, 3:4]).then_inc(xch_ok, 1)
                nc.scalar.activation(xcT[s][:], gc[s][:], ACT.Relu, bias=bn_fac[:, 3:4]).then_inc(xc_ok, 1)

            def gather_out(pair, s, first):
                act.wait_ge(nm_mm, after(pair, s))
                if not first:
                    act.wait_ge(in_mm, after(pair - 1, s))
                nc.scalar.activation(nmh[s][:], bank(2 + s), ACT.Copy).then_inc(nmh_ok, 1)

            def gates_out(pair, s, first):
                act.wait_ge(r_mm, after(pair, s))
                if not first:
                    act.wait_ge(y1_ok, after(pair - 1, s))
                nc.scalar.activation(tr[s][:], bank(0), ACT.Tanh, bias=gbias[:, 0:1], scale=0.5).then_inc(tr_ok, 1)
                act.wait_ge(z_mm, after(pair, s))
                nc.scalar.activation(tz[s][:], bank(1), ACT.Tanh, bias=gbias[:, 1:2], scale=0.5).then_inc(tz_ok, 1)

            def new_state(pair, s):
                act.wait_ge(q2_ok, after(pair, s))
                nc.scalar.activation(nT[s][:], q2[s][:], ACT.Tanh, bias=bih[:, 2:3]).then_inc(n_ok, 1)

            def degree(pair, s):
                act.wait_ge(adjN_in[s], loaded(pair))
                for b in range(NB):
                    i = nc.scalar.activation(adjN[s][:, b, :], adjN[s][:, b, :], ACT.Copy, accum_out=deg[s][:, b:b + 1])
                i.then_inc(deg_ok, 1)

            def body(pair, first=False, last=False):
                conv1_out(pair, 0, first)
                embed_out(pair, 0, first)
                message_out(pair, 0)
                x1_out(pair, 1, first)
                exps(pair, 0, first)
                conv1_out(pair, 1, first)
                embed_out(pair, 1, first)
                conv2_out(pair, 0, first)
                message_out(pair, 1)
                if not last:
                    degree(pair + 1, 0)
                exps(pair, 1, first)
                if not last:
                    degree(pair + 1, 1)
                conv2_out(pair, 1, first)
                gather_out(pair, 0, first)
                gather_out(pair, 1, first)
                gates_out(pair, 0, first)
                new_state(pair, 0)
                gates_out(pair, 1, first)
                if not last:
                    x1_out(pair + 1, 0, False)
                new_state(pair, 1)

            degree(0, 0)
            degree(0, 1)
            act.wait_ge(w_in, WEIGHTS_IN)
            for dst, src in ((w1h, w1), (w2h, w2), (wihh, wih), (whhh, whh)):
                nc.scalar.activation(dst[:], src, ACT.Copy).then_inc(w_hi, 1)
            act.wait_ge(rep_ok, 2)
            nc.scalar.activation(wseh[:], wse_rep[:], ACT.Copy).then_inc(w_hi, 1)
            act.wait_ge(fold_ok, 1)
            x1_out(0, 0, True)
            pair_loop(act, lambda p: body(p, first=True), body, lambda p: body(p, last=True))

        @block.vector
        def _(dve):
            def bcast(v):
                return v[:].unsqueeze(2).to_broadcast([P, NB, D])

            def rows(v):
                return v[:].unsqueeze(1).to_broadcast([P, NB, D])

            def v3(x):
                return x.rearrange("p (b d) -> p b d", b=NB)

            def norm(pair, s, src, st, m, rs, dst, ready, st_ok, mv_ok, rs_ok, rstd_ok, dst_ok, dst_free):
                dve.wait_ge(*ready)
                for b in range(NB):
                    i = nc.vector.bn_stats(st[s][:, b, :], src[:, b, :])
                dve.drain()
                for b in range(NB):
                    i = nc.vector.bn_aggr(m[s][:, b, :], st[s][:, b, :])
                i.then_inc(mv_ok, 1)
                dve.wait_ge(mv_ok, after(pair, s))
                nc.vector.tensor_scalar(rs[s][:], m[s][:, :, 1], EPS, None, ALU.add).then_inc(rs_ok, 1)
                dve.wait_ge(rstd_ok, after(pair, s))
                if dst_free is not None:
                    dve.wait_ge(*dst_free)
                for b in range(NB):
                    i = nc.vector.tensor_scalar(dst[s][:, b, :], src[:, b, :], m[s][:, b, 0:1], rs[s][:, b:b + 1],
                                                ALU.subtract, ALU.mult)
                i.then_inc(dst_ok, 1)

            def degree(pair, s):
                dve.wait_ge(deg_ok, after(pair, s))
                nc.vector.tensor_scalar(deg[s][:], deg[s][:], 1.0, None, ALU.add).then_inc(deg1_ok, 1)

            def scale_in(pair, s):
                dve.wait_ge(dinv_ok, after(pair, s))
                dve.wait_ge(y_mm, after(pair, s))
                nc.vector.tensor_tensor(yd[s][:], v3(bank(4 + 2 * s)), bcast(dinv[s]), ALU.mult).then_inc(yd_ok, 1)

            def first_layer_out(pair, s):
                dve.wait_ge(l0_mm, after(pair, s))
                nc.vector.tensor_tensor(z1[s][:], v3(bank(5 + 2 * s)), yd[s][:], ALU.add).then_inc(z1_ok, 1)

            def first_layer_norm(pair, s):
                dve.wait_ge(z3_ok, after(pair, s))
                dve.wait_ge(xN_in[s], loaded(pair))
                nc.vector.scalar_tensor_tensor(y0[s][:].rearrange("p b d -> p (b d)"), z3[s][:].rearrange("p b d -> p (b d)"), 0.0, xN[s][:].rearrange("p b d -> p (b d)"), ALU.max, ALU.add).then_inc(y0_ok, 1)
                norm(pair, s, y0[s], stats, mv, rstd, x1N, (y0_ok, after(pair, s)), st_ok, mv_ok, rs_ok, rstd_ok, x1N_ok, None)

            def x1_lo(pair, s, first):
                dve.wait_ge(x1h_ok, after(pair, s))
                dve.wait_ge(x1T_ok, after(pair, s))
                nc.vector.tensor_tensor(x1l[s][:], x1T[s][:], x1h[s][:].bitcast(FP32), ALU.subtract).then_inc(x1l_ok, 1)

            def h_lo(pair, s):
                dve.wait_ge(hh_ok, after(pair, s))
                nc.vector.tensor_tensor(hl[s][:, HALO:HALO + N], hT[s][:], hh[s][:, HALO:HALO + N].bitcast(FP32), ALU.subtract).then_inc(hl_ok, 1)

            def dist_operands(pair, s):
                dve.wait_ge(sqr_ok, after(pair, s))
                dve.wait_ge(slin_ok, after(pair, s))
                nc.vector.scalar_tensor_tensor(su[s][:], sqr[s][:], coef[:, 0:1], slin[s][:], ALU.mult, ALU.add).then_inc(su_ok, 1)
                dve.wait_ge(su_ok, after(pair, s))
                nc.vector.tensor_copy(suh[s][:], su[s][:]).then_inc(suh_ok, 1)
                nc.vector.tensor_scalar(suR[s][:], su[s][:], coef[:, 3:4], coef[:, 4:5], ALU.mult, ALU.add).then_inc(suR_ok, 1)
                nc.vector.tensor_scalar(suL[s][:], su[s][:], coef[:, 6:7], coef[:, 7:8], ALU.mult, ALU.add).then_inc(suL_ok, 1)
                dve.wait_ge(suh_ok, after(pair, s))
                dve.wait_ge(suR_ok, after(pair, s))
                nc.vector.scalar_tensor_tensor(dR[s][:], suh[s][:].bitcast(FP32), coef[:, 2:3], suR[s][:], ALU.mult, ALU.add).then_inc(dR_ok, 1)
                dve.wait_ge(suL_ok, after(pair, s))
                nc.vector.scalar_tensor_tensor(dL[s][:], suh[s][:].bitcast(FP32), coef[:, 5:6], suL[s][:], ALU.mult, ALU.add).then_inc(dL_ok, 1)

            def message_out(pair, s, first):
                dve.wait_ge(msg_mm, after(pair, s))
                if not first:
                    dve.wait_ge(nm_mm, after(pair - 1, s))
                nc.vector.tensor_tensor(mb_[s][:], v3(bank(2 + s)), rows(bmsg_rep), ALU.add).then_inc(mb_ok, 1)

            def mask(pair, s):
                dve.wait_ge(exp_ok, after(pair, s))
                nc.vector.tensor_tensor(em[s], em[s], adjT[s][:], ALU.mult).then_inc(em_ok, 1)

            def conv2_out(pair, s):
                dve.wait_ge(c2_mm, after(pair, s))
                nc.vector.scalar_tensor_tensor(gc[s][:], bank(s), bn_fac[:, 2:3], x1T[s][:], ALU.mult, ALU.add).then_inc(gc_ok, 1)

            def xc_lo(pair, s):
                dve.wait_ge(xc_ok, after(pair, s))
                dve.wait_ge(xch_ok, after(pair, s))
                nc.vector.tensor_tensor(xcl[s][:], xcT[s][:], xch[s][:].bitcast(FP32), ALU.subtract).then_inc(xcl_ok, 1)

            def nm_lo(pair, s):
                dve.wait_ge(nmh_ok, after(pair, s))
                nc.vector.tensor_tensor(nml[s][:], bank(2 + s), nmh[s][:].bitcast(FP32), ALU.subtract).then_inc(nml_ok, 1)

            def gates_out(pair, s):
                dve.wait_ge(tr_ok, after(pair, s))
                nc.vector.tensor_scalar(tr1[s][:], tr[s][:], 1.0, 0.5, ALU.add, ALU.mult).then_inc(tr1_ok, 1)
                dve.wait_ge(tr1_ok, after(pair, s))
                dve.wait_ge(hn_mm, after(pair, s))
                nc.vector.scalar_tensor_tensor(q1[s][:], bank(2), bhh[:, 2:3], tr1[s][:], ALU.add, ALU.mult).then_inc(q1_ok, 1)
                dve.wait_ge(q1_ok, after(pair, s))
                dve.wait_ge(in_mm, after(pair, s))
                nc.vector.tensor_tensor(q2[s][:], bank(3), q1[s][:], ALU.add).then_inc(q2_ok, 1)

            def state_out(pair, s):
                dve.wait_ge(e1_ok, after(pair, s))
                nc.vector.scalar_tensor_tensor(e2[s][:], tz[s][:], 1.0, e1[s][:], ALU.add, ALU.mult).then_inc(e2_ok, 1)
                dve.wait_ge(e2_ok, after(pair, s))
                dve.wait_ge(e3_ok, after(pair, s))
                nc.vector.scalar_tensor_tensor(y1[s][:], e2[s][:], 0.5, e3[s][:], ALU.mult, ALU.add).then_inc(y1_ok, 1)

            def second_norm(pair, s, stored):
                free = (out_stored[s], 16 * stored) if stored is not None else None
                norm(pair, s, v3(bank(2 + s)), stats1, mv1, rstd1, outN, (y1_mm, after(pair, s)), st1_ok, mv1_ok, rs1_ok,
                     rstd1_ok, out_ok, free)

            def body(pair, first=False, last=False, stored=None):
                h_lo(pair, 0)
                message_out(pair, 0, first)
                dist_operands(pair, 0)
                first_layer_norm(pair, 1)
                x1_lo(pair, 1, first)
                mask(pair, 0)
                conv2_out(pair, 0)
                h_lo(pair, 1)
                dist_operands(pair, 1)
                message_out(pair, 1, first)
                xc_lo(pair, 0)
                if not last:
                    degree(pair + 1, 0)
                if not first:
                    second_norm(pair - 1, 0, stored)
                mask(pair, 1)
                if not first:
                    second_norm(pair - 1, 1, stored)
                if not last:
                    degree(pair + 1, 1)
                conv2_out(pair, 1)
                xc_lo(pair, 1)
                if not last:
                    for s in range(2):
                        scale_in(pair + 1, s)
                nm_lo(pair, 0)
                nm_lo(pair, 1)
                if not last:
                    first_layer_out(pair + 1, 0)
                gates_out(pair, 0)
                if not last:
                    first_layer_norm(pair + 1, 0)
                state_out(pair, 0)
                gates_out(pair, 1)
                if not last:
                    x1_lo(pair + 1, 0, False)
                state_out(pair, 1)
                if not last:
                    first_layer_out(pair + 1, 1)

            nc.vector.memset(wse_rep[:], 0.0).then_inc(rep_ok, 1)
            dve.wait_ge(w_in, WEIGHTS_IN)
            dve.wait_ge(rep_ok, 1)
            nc.vector.tensor_copy(wse_rep[:, 0:DIST_ROWS].rearrange("p (a b) -> p a b", b=SE),
                                  wseT[:].unsqueeze(1).to_broadcast([P, DIST_ROWS // SE, SE])).then_inc(rep_ok, 1)
            bn4 = bn[:].rearrange("p (l k) -> p k l", l=2)
            fac = bn_fac[:].rearrange("p (l k) -> p k l", l=2)
            nc.vector.tensor_scalar(bn_tmp[:, 0:2], bn4[:, 3, :], EPS, None, ALU.add).then_inc(fold_var, 1)
            nc.vector.tensor_tensor(gbias2[:, 0:2], bih[:, 0:2], bhh[:, 0:2], ALU.add).then_inc(fold_step, 1)
            nc.vector.tensor_tensor(bse_lin[:], bse_col[:], coef[:, 1:2], ALU.mult).then_inc(fold_step, 1)
            dve.wait_ge(fold_step, 2)
            dve.wait_ge(fold_pow, 1)
            nc.vector.tensor_tensor(fac[:, 0, :], bn4[:, 0, :], bn_tmp[:, 0:2], ALU.mult).then_inc(fold_step, 1)
            nc.vector.tensor_scalar(gbias[:, 0:2], gbias2[:, 0:2], 0.5, None, ALU.mult).then_inc(fold_step, 1)
            dve.wait_ge(fold_step, 4)
            nc.vector.tensor_tensor(bn_tmp[:, 2:4], bn4[:, 2, :], fac[:, 0, :], ALU.mult).then_inc(fold_step, 1)
            dve.wait_ge(fold_step, 5)
            nc.vector.tensor_tensor(fac[:, 1, :], bn4[:, 1, :], bn_tmp[:, 2:4], ALU.subtract).then_inc(fold_ok, 1)
            for i, (lo, whole, hi) in enumerate(((w1l, w1, w1h), (w2l, w2, w2h), (wihl, wih, wihh), (whhl, whh, whhh),
                                                 (wsel, wse_rep[:], wseh))):
                dve.wait_ge(w_hi, i + 1)
                nc.vector.tensor_tensor(lo[:], whole, hi[:].bitcast(FP32), ALU.subtract).then_inc(w_lo, 1)
            for s in range(2):
                degree(0, s)
            for s in range(2):
                scale_in(0, s)
            first_layer_out(0, 0)
            first_layer_out(0, 1)
            first_layer_norm(0, 0)
            x1_lo(0, 0, True)
            body(0, first=True)
            body(1, stored=None)
            with dve.Fori(2, PAIRS - 1) as pair:
                body(pair, stored=pair - 1)
            body(PAIRS - 1, last=True, stored=PAIRS - 2)
            for s in range(2):
                second_norm(PAIRS - 1, s, PAIRS - 1)

        @block.gpsimd
        def _(pool):
            def rsqrt(tile, ready, done):
                pool.wait_ge(*ready)
                nc.gpsimd.tensor_tensor(tile, tile, neg_half[:, 0:tile.shape[1]], ALU.pow).then_inc(done, 1)

            def degrees(pair, s):
                pool.wait_ge(deg1_ok, after(pair, s))
                nc.gpsimd.tensor_tensor(dinv[s][:], deg[s][:], neg_half[:], ALU.pow).then_inc(dinv_ok, 1)

            def first_layer_out(pair, s):
                pool.wait_ge(z1_ok, after(pair, s))
                nc.gpsimd.tensor_tensor(z2[s][:], z1[s][:], dinv[s][:].unsqueeze(2).to_broadcast([P, NB, D]), ALU.mult).then_inc(z2_ok, 1)
                pool.wait_ge(z2_ok, after(pair, s))
                nc.gpsimd.tensor_tensor(z3[s][:], z2[s][:], b0_rep[:].unsqueeze(1).to_broadcast([P, NB, D]), ALU.add).then_inc(z3_ok, 1)

            def gates_out(pair, s, first):
                pool.wait_ge(n_ok, after(pair, s))
                if not first:
                    pool.wait_ge(y1_mm, after(pair - 1, s))
                nc.gpsimd.tensor_tensor(e1[s][:], x1T[s][:], nT[s][:], ALU.subtract).then_inc(e1_ok, 1)
                nc.gpsimd.tensor_tensor(e3[s][:], x1T[s][:], nT[s][:], ALU.add).then_inc(e3_ok, 1)

            def body(pair, first=False, last=False):
                rsqrt(rstd[1][:], (rs_ok, after(pair, 1)), rstd_ok)
                if not last:
                    degrees(pair + 1, 0)
                if not first:
                    for s in range(2):
                        rsqrt(rstd1[s][:], (rs1_ok, after(pair - 1, s)), rstd1_ok)
                if not last:
                    degrees(pair + 1, 1)
                    first_layer_out(pair + 1, 0)
                    rsqrt(rstd[0][:], (rs_ok, after(pair + 1, 0)), rstd_ok)
                gates_out(pair, 0, first)
                gates_out(pair, 1, first)
                if not last:
                    first_layer_out(pair + 1, 1)

            nc.gpsimd.memset(bse_col[:], 0.0).then_inc(bse_zero, 1)
            nc.gpsimd.memset(neg_half[:], -0.5).then_inc(half_ok, 1)
            for tile in hh + hl:
                halos = tile[:].bitcast(FP32)
                nc.gpsimd.memset(halos[:, 0:HALO], 0.0)
                nc.gpsimd.memset(halos[:, HALO + N:N + 2 * HALO], 0.0).then_inc(halo_ok, 1)
            pool.wait_ge(half_ok, 1)
            rsqrt(bn_tmp[:, 0:2], (fold_var, 1), fold_pow)
            for s in range(2):
                degrees(0, s)
            for s in range(2):
                first_layer_out(0, s)
            rsqrt(rstd[0][:], (rs_ok, after(0, 0)), rstd_ok)
            pair_loop(pool, lambda p: body(p, first=True), body, lambda p: body(p, last=True))
            for s in range(2):
                rsqrt(rstd1[s][:], (rs1_ok, after(PAIRS - 1, s)), rstd1_ok)


def kernel(**inputs):
    import numpy as np
    from concourse import bacc
    from concourse.bass_utils import run_bass_kernel_spmd

    a = {k: np.asarray(v) for k, v in inputs.items()}
    L = {k[len("L1_gnn_"):]: v for k, v in a.items() if k.startswith("L1_gnn_")}
    arrays = {
        "adjN": a["adj"], "adjT": a["adj"].transpose(0, 2, 1), "xN": a["x"], "xT": a["x"].transpose(0, 2, 1),
        "w0T": a["L0_gnn_W"].T, "b0": a["L0_gnn_b"], "wmsgT": L["w_msg"].T, "bmsg": L["b_msg"],
        "wseT": L["w_se"].T, "bse": L["b_se"], "w1T": L["conv1_w"][:, :, 0].T, "w2T": L["conv2_w"].transpose(1, 2, 0),
        "wihT": L["w_ih"].T, "whhT": L["w_hh"].T, "bih": L["b_ih"].reshape(3, D).T, "bhh": L["b_hh"].reshape(3, D).T,
        "bn": np.stack([L[f"bn{i}_{k}"] for i in (1, 2) for k in "gbmv"], axis=1),
        "ident": np.eye(P, dtype=np.float32), "coef": distance_factors(),
    }
    arrays = {f"in_{k}": np.ascontiguousarray(v) for k, v in arrays.items()}
    nc = bacc.Bacc("TRN2", target_bir_lowering=False, num_devices=1)
    t = {k[3:]: nc.dram_tensor(k, v.shape, mybir.dt.from_np(v.dtype), kind="ExternalInput").ap() for k, v in arrays.items()}
    out = nc.dram_tensor("out", (G, N, D), FP32, kind="ExternalOutput").ap()
    gnn_kernel(nc, t, out)
    r = run_bass_kernel_spmd(nc, [arrays], core_ids=[0])
    return r.results[0]["out"]
```

```python
from contextlib import ExitStack

import concourse.bass as bass
from concourse import mybir

FP32 = mybir.dt.float32
FP32R = mybir.dt.float32r
ACT = mybir.ActivationFunctionType
ALU = mybir.AluOpType

G, N, D, TAPS, SE = 16, 512, 128, 17, 3
P = 128
NB = N // P
PAIRS = G // 2
HALO = TAPS // 2
TAP_GROUPS = -(-TAPS // 3)
PRODUCTS = (TAP_GROUPS,) * 3 + (TAPS // 3,)
PADDED = N + 2 * HALO + 2
WIN = N + 2 * HALO
EPS = 1e-5
COLUMNS = {"wmsgT": D, "wseT": SE, "coef": 8, "bih": 3, "bhh": 3, "bn": 8}
DIST_ROWS = 8 * SE


def distance_factors():
    import numpy as np
    hi, lo, minus = (1, 0, 0), (-1, 1, 0), (0, 0, -1)
    twice = lambda f: tuple(2 * x for x in f)
    kinds = [(0, hi, twice(hi)), (0, lo, twice(hi)), (0, hi, twice(lo)), (0, lo, twice(lo)),
             (1, hi, minus), (1, lo, minus), (1, minus, hi), (1, minus, lo)]
    f = np.zeros((P, 8), np.float32)
    for i, (square, moving, stationary) in enumerate(kinds):
        f[SE * i:SE * (i + 1)] = (square, 1 - square) + moving + stationary
    return f


def after(pair, slot):
    return pair * 2 + (slot + 1)


def loaded(pair):
    return (pair + 1) * 16


def of_pair(pair, step, steps):
    return pair * steps + (step + 1)


def gnn_kernel(nc, t, out):
    ctx = ExitStack()
    with ctx:
        def sb(name, shape, dt=FP32):
            return ctx.enter_context(nc.sbuf_tensor(name, shape, dt))

        def sem(name):
            return ctx.enter_context(nc.semaphore(name))

        first_weights = sb("first_weights", [P, D + P])
        w0T, ident = first_weights[:, 0:D], first_weights[:, D:D + P]
        b0_rep = sb("b0_rep", [P, D])
        bmsg_rep = sb("bmsg_rep", [P, D])
        columns = sb("columns", [P, sum(COLUMNS.values())])
        at = {k: sum(list(COLUMNS.values())[:i]) for i, k in enumerate(COLUMNS)}
        wmsgT, wseT, coef, bih, bhh, bn = (columns[:, at[k]:at[k] + n] for k, n in COLUMNS.items())
        wse_rep = sb("wse_rep", [P, P])
        bse_col = sb("bse_col", [P, 1])
        bse_lin = sb("bse_lin", [P, 1])
        w1h, w1l = sb("w1h", [P, D], FP32R), sb("w1l", [P, D], FP32R)
        w2h, w2l = sb("w2h", [P, sum(PRODUCTS), D], FP32R), sb("w2l", [P, sum(PRODUCTS), D], FP32R)
        wihh, wihl = sb("wihh", [P, 2, 3 * D], FP32R), sb("wihl", [P, 2, 3 * D], FP32R)
        whhh, whhl = sb("whhh", [P, 3 * D], FP32R), sb("whhl", [P, 3 * D], FP32R)
        wseh, wsel = sb("wseh", [P, P], FP32R), sb("wsel", [P, P], FP32R)
        bn_fac = sb("bn_fac", [P, 4])
        bn_tmp = sb("bn_tmp", [P, 4])
        bn_minus = sb("bn_minus", [P, 1])
        gbias2 = sb("gbias2", [P, 2])
        gbias = sb("gbias", [P, 2])
        neg_half = sb("neg_half", [P, NB])

        def two(name, shape, dt=FP32):
            return [sb(f"{name}{s}", shape, dt) for s in range(2)]

        adjT = two("adjT", [P, NB, N])
        adjN = sb("adjN", [P, NB, N])
        xT = two("xT", [P, N])
        xN = two("xN", [P, NB, D])
        deg = two("deg", [P, NB])
        dinv = two("dinv", [P, NB])
        yd = outN = two("yd", [P, NB, D])
        z1 = z2 = z3 = y0 = x1N = two("x1N", [P, NB, D])
        stats, stats1 = two("stats", [P, NB, 6]), two("stats1", [P, NB, 6])
        mv, mv1 = two("mv", [P, NB, 2]), two("mv1", [P, NB, 2])
        rstd, rstd1 = two("rstd", [P, NB]), two("rstd1", [P, NB])
        shift, shift1 = two("shift", [P, NB]), two("shift1", [P, NB])
        x1T_pair = [sb(f"x1T_{par}", [P, 2, N]) for par in range(2)]
        x1h_pair = [sb(f"x1h_{par}", [P, 2, N], FP32R) for par in range(2)]
        x1l_pair = [sb(f"x1l_{par}", [P, 2, N], FP32R) for par in range(2)]
        x1T = [[v[:, s] for s in range(2)] for v in x1T_pair]
        x1h = [[v[:, s] for s in range(2)] for v in x1h_pair]
        x1l = [[v[:, s] for s in range(2)] for v in x1l_pair]
        hT = two("hT", [P, PADDED])
        diff2, sum1, diff1 = two("diff2", [P, WIN]), two("sum1", [P, WIN]), two("diff1", [P, WIN])
        diff2h, diff2l, sum1h, sum1l, diff1h, diff1l = (
            sb(name, [P, 2, 2, WIN // 2], FP32R) for name in "diff2h diff2l sum1h sum1l diff1h diff1l".split())
        sqr = su = suL = two("suL", [P, N])
        slin = suR = two("suR", [P, N])
        suh = sb("suh", [P, N], FP32R)
        dR, dL = two("dR", [P, N], FP32R), two("dL", [P, N], FP32R)
        mb_ = msg = two("msg", [P, NB, D])
        em_both = sb("em", [P, 2, NB, N])
        em = [em_both[:, s] for s in range(2)]
        gc_pair = sb("gc", [P, 2, N])
        gc = xcT = [gc_pair[:, s] for s in range(2)]
        xch, xcl = two("xch", [P, N], FP32R), two("xcl", [P, N], FP32R)
        nmh, nml = dR, dL
        gate_tiles = sb("gate_tiles", [P, 3, 2, N])
        tr = tr1 = q1 = q2 = nT = minus_new = [gate_tiles[:, 0, s] for s in range(2)]
        tz = [gate_tiles[:, 1, s] for s in range(2)]
        kept_factor = kept = y1 = [gate_tiles[:, 2, s] for s in range(2)]

        early = em_both[:].rearrange("p s b n -> p (s b n)")
        w2 = early[:, 0:3 * TAP_GROUPS * D].rearrange("p (k o) -> p k o", o=D)
        at = 3 * TAP_GROUPS * D
        w2_plus = early[:, at:at + TAP_GROUPS * D].rearrange("p (k o) -> p k o", o=D)
        early = gate_tiles[:].rearrange("p a s n -> p (a s n)")
        staged = early[:, 0:10 * D]
        wih = early[:, 0:6 * D].rearrange("p (k o) -> p k o", k=2)
        whh, w1 = early[:, 6 * D:9 * D], early[:, 9 * D:10 * D]
        w2_minus = early[:, 10 * D:16 * D].rearrange("p (k o) -> p k o", o=D)

        ps = ctx.enter_context(nc.psum_tensor("ps", [P, 8, N], FP32))

        X1_BANK, MSG_BANK, Y1_BANK, ADJ_BANK, Y_BANK = (4, 5), (4, 5), (6, 3), (4, 5), (4, 5)
        CONV1_BANK, EMBED_BANK, GATHER_BANK = 6, 7, (6, 7)
        GATE_R, GATE_Z, GATE_HN, GATE_IN = range(4)

        def bank(i):
            return ps[:, i, :]

        first_in, columns_in, staged_in, taps_in = sem("first_in"), sem("columns_in"), sem("staged_in"), sem("taps_in")
        b0_in, bmsg_in, bse_in = sem("b0_in"), sem("bmsg_in"), sem("bse_in")
        wse_ok, taps_step, w_hi, w_lo = sem("wse_ok"), sem("taps_step"), sem("w_hi"), sem("w_lo")
        fold_ok, fold_step = sem("fold_ok"), sem("fold_step")
        half_ok, fold_var, fold_pow = sem("half_ok"), sem("fold_var"), sem("fold_pow")
        halo_ok, bse_zero, tap_zero = sem("halo_ok"), sem("bse_zero"), sem("tap_zero")
        adjN_in = sem("adjN_in")
        adjT_in = [sem(f"adjT_in{s}") for s in range(2)]
        xT_in = [sem(f"xT_in{s}") for s in range(2)]
        xN_in = [sem(f"xN_in{s}") for s in range(2)]
        out_stored = [sem(f"out_stored{s}") for s in range(2)]
        deg_ok, deg1_ok, dinv_ok, y_mm, yd_ok, l0_mm, z1_ok, z2_ok, z3_ok, y0_ok = (sem(x) for x in (
            "deg_ok deg1_ok dinv_ok y_mm yd_ok l0_mm z1_ok z2_ok z3_ok y0_ok").split())
        mv_ok, var_ok, rstd_ok, shift_ok, x1N_ok = (sem(x) for x in "mv_ok var_ok rstd_ok shift_ok x1N_ok".split())
        x1_mm, x1T_ok, x1h_ok, x1l_ok, c1_mm, h_ok, s_mm, sqr_ok, slin_ok, msg_mm, mb_ok, msg_ok = (sem(x) for x in (
            "x1_mm x1T_ok x1h_ok x1l_ok c1_mm h_ok s_mm sqr_ok slin_ok msg_mm mb_ok msg_ok").split())
        diff2_ok, diff2h_ok, diff2l_ok, sum1_ok, sum1h_ok, sum1l_ok, diff1_ok, diff1h_ok, diff1l_ok = (sem(x) for x in (
            "diff2_ok diff2h_ok diff2l_ok sum1_ok sum1h_ok sum1l_ok diff1_ok diff1h_ok diff1l_ok").split())
        su_ok, suh_ok, suR_ok, suL_ok, dR_ok, dL_ok, dist_mm, exp_ok, em_ok, nm_mm, nmh_ok, nml_ok = (sem(x) for x in (
            "su_ok suh_ok suR_ok suL_ok dR_ok dL_ok dist_mm exp_ok em_ok nm_mm nmh_ok nml_ok").split())
        c2_mm, gc_step, xch_ok, xc_ok, xcl_ok = (sem(x) for x in "c2_mm gc_step xch_ok xc_ok xcl_ok".split())
        r_mm, z_mm, hn_mm, in_mm, tr_ok, tz_ok, tr1_ok, q1_ok, q2_ok, n_ok, factor_ok, kept_ok, minus_ok, y1_ok, y1_mm = (
            sem(x) for x in "r_mm z_mm hn_mm in_mm tr_ok tz_ok tr1_ok q1_ok q2_ok n_ok factor_ok kept_ok minus_ok y1_ok y1_mm".split())
        mv1_ok, var1_ok, rstd1_ok, shift1_ok, out_ok = (sem(x) for x in "mv1_ok var1_ok rstd1_ok shift1_ok out_ok".split())

        w2_halves = [[v[:, sum(PRODUCTS[:i]):sum(PRODUCTS[:i + 1]), :] for v in (w2h, w2l)] for i in range(4)]
        weight_halves = [
            ((w1h[:], w1l[:]), w1, 1.0), ((wseh[:], wsel[:]), wse_rep[:], 1.0),
            (w2_halves[0], w2[:, 0::3, :], 1.0), (w2_halves[1], w2_plus, 0.5), (w2_halves[2], w2_minus, 0.5),
            (w2_halves[3], w2[:, 2:TAPS:3, :], -1.0),
            ((wihh[:], wihl[:]), wih, 1.0), ((whhh[:], whhl[:]), whh, 1.0)]
        X1_WEIGHTS, CONV2_WEIGHTS, GATE_WEIGHTS = 2, 6, len(weight_halves)

        block = ctx.enter_context(nc.Block())

        def pair_loop(eng, body):
            body(0, 0, first=True)
            with eng.Fori(1, PAIRS - 2, 2) as pair:
                body(pair, 1)
                body(pair + 1, 0)
            body(PAIRS - 1, 1, last=True)

        @block.sync
        def _(sync):
            def load_features(pair, s, reuse):
                g = bass.ds(pair * 2 + s, 1)
                if reuse:
                    sync.wait_ge(y_mm, after(pair - 1, s))
                sync.dma_start(xT[s][:], t["xT"][g].rearrange("a p n -> p (a n)")).then_inc(xT_in[s], 16)

            def load_nodes(pair, s, reuse):
                g = bass.ds(pair * 2 + s, 1)
                if reuse:
                    sync.wait_ge(y0_ok, after(pair - 1, s))
                sync.dma_start(xN[s][:], t["xN"][g].rearrange("a (b p) n -> p (a b) n", p=P)).then_inc(xN_in[s], 16)

            def load_degrees(pair, s, reuse):
                if reuse:
                    sync.wait_ge(deg_ok, pair * 2 + s)
                sync.dma_start(adjN[:], t["adjN"][bass.ds(pair * 2 + s, 1)].rearrange("a (b p) n -> p (a b) n", p=P)).then_inc(adjN_in, 16)

            def load_edges(pair, s, reuse):
                if reuse:
                    sync.wait_ge(em_ok, after(pair - 1, s))
                sync.dma_start(adjT[s][:], t["adjT"][bass.ds(pair * 2 + s, 1)].rearrange("a (b p) n -> p (a b) n", p=P)).then_inc(adjT_in[s], 16)

            def store(pair, s):
                sync.wait_ge(out_ok, after(pair, s))
                sync.dma_start(out[bass.ds(pair * 2 + s, 1)].rearrange("a (b p) d -> p (a b) d", p=P), outN[s][:]).then_inc(out_stored[s], 16)

            def body(pair, par, first=False, last=False):
                if not last:
                    load_degrees(pair + 1, 0, True)
                    for s in range(2):
                        load_features(pair + 1, s, True)
                        load_nodes(pair + 1, s, True)
                    load_degrees(pair + 1, 1, True)
                if not first:
                    store(pair - 1, 0)
                    store(pair - 1, 1)
                if not last:
                    load_edges(pair + 1, 0, True)
                    load_edges(pair + 1, 1, True)

            sync.dma_start(first_weights[:], t["first_weights"]).then_inc(first_in, 16)
            load_degrees(0, 0, False)
            load_features(0, 0, False)
            load_edges(0, 0, False)
            load_features(0, 1, False)
            load_degrees(0, 1, True)
            sync.dma_start(columns[:], t["columns"]).then_inc(columns_in, 16)
            sync.dma_start(b0_rep[:], t["b0"].partition_broadcast(P)).then_inc(b0_in, 16)
            load_nodes(0, 0, False)
            load_edges(0, 1, False)
            sync.dma_start(staged, t["staged"]).then_inc(staged_in, 16)
            sync.wait_ge(bse_zero, 1)
            sync.dma_start(bse_col[0:DIST_ROWS, :], t["bse"]).then_inc(bse_in, 16)
            load_nodes(0, 1, False)
            sync.dma_start(w2[:, 0:TAPS, :], t["w2T"]).then_inc(taps_in, 16)
            sync.dma_start(bmsg_rep[:], t["bmsg"].partition_broadcast(P)).then_inc(bmsg_in, 16)
            pair_loop(sync, body)
            for s in range(2):
                store(PAIRS - 1, s)
            for s in range(2):
                sync.wait_ge(out_stored[s], 16 * PAIRS)

        @block.tensor
        def _(pe):
            def split3(o, wh, wl, parts, start, stop):
                nc.tensor.matmul(o, wh, parts[0], start=start, stop=False)
                nc.tensor.matmul(o, wh, parts[1], start=False, stop=False)
                return nc.tensor.matmul(o, wl, parts[0], start=False, stop=stop)

            def first_layer_in(pair, s):
                pe.wait_ge(xT_in[s], loaded(pair))
                for b in range(NB):
                    mm = nc.tensor.matmul(bank(Y_BANK[s])[:, b * D:(b + 1) * D], xT[s][:, b * P:(b + 1) * P], w0T,
                                          start=True, stop=True)
                mm.then_inc(y_mm, 1)

            def first_layer_adj(pair, s):
                pe.wait_ge(adjT_in[s], loaded(pair))
                pe.wait_ge(yd_ok, after(pair, s))
                for nb in range(NB):
                    for mb in range(NB):
                        mm = nc.tensor.matmul(bank(ADJ_BANK[s])[:, nb * D:(nb + 1) * D], adjT[s][:, mb, nb * P:(nb + 1) * P],
                                              yd[s][:, mb, :], start=mb == 0, stop=mb == NB - 1)
                mm.then_inc(l0_mm, 1)

            def transpose_x1(pair, s):
                pe.wait_ge(x1N_ok, after(pair, s))
                for b in range(NB):
                    mm = nc.tensor.transpose(bank(X1_BANK[s])[:, b * P:(b + 1) * P], x1N[s][:, b, :], ident)
                mm.then_inc(x1_mm, 1)

            def conv1(pair, par, s, first):
                pe.wait_ge(x1h_ok, after(pair, s))
                pe.wait_ge(x1l_ok, after(pair, s))
                if s == 0 and not first:
                    pe.wait_ge(nml_ok, after(pair - 1, 1))
                    pe.wait_ge(nmh_ok, after(pair - 1, 1))
                if s == 1:
                    pe.wait_ge(h_ok, after(pair, 0))
                split3(bank(CONV1_BANK), w1h[:], w1l[:], (x1h[par][s], x1l[par][s]), True, True).then_inc(c1_mm, 1)

            def embed(pair, par, s):
                if s == 1:
                    pe.wait_ge(sqr_ok, after(pair, 0))
                    pe.wait_ge(slin_ok, after(pair, 0))
                split3(bank(EMBED_BANK), wseh[:], wsel[:], (x1h[par][s], x1l[par][s]), True, True).then_inc(s_mm, 1)

            def messages(pair, par, s):
                pe.wait_ge(x1T_ok, after(pair, s))
                for b in range(NB):
                    mm = nc.tensor.matmul(bank(MSG_BANK[s])[:, b * D:(b + 1) * D], x1T[par][s][:, b * P:(b + 1) * P], wmsgT,
                                          start=True, stop=True)
                mm.then_inc(msg_mm, 1)

            def conv2(pair, product, first):
                hi, lo, hi_ok, lo_ok, offset = (
                    (diff2h, diff2l, diff2h_ok, diff2l_ok, 0), (sum1h, sum1l, sum1h_ok, sum1l_ok, 1),
                    (diff1h, diff1l, diff1h_ok, diff1l_ok, 1), (diff2h, diff2l, diff2h_ok, diff2l_ok, 1))[product]
                pe.wait_ge(hi_ok, after(pair, 1))
                pe.wait_ge(lo_ok, after(pair, 1))
                if first:
                    pe.wait_ge(w_hi, X1_WEIGHTS + product + 1)
                    pe.wait_ge(w_lo, X1_WEIGHTS + product + 1)
                else:
                    pe.wait_ge((tr_ok, tz_ok, q1_ok, out_ok)[product], after(pair - 1, 1))
                o = bank(product).rearrange("p (s t) -> p s t", s=2)
                for g in range(PRODUCTS[product]):
                    odd, at = (3 * g + offset) % 2, (3 * g + offset) // 2
                    w = sum(PRODUCTS[:product]) + g
                    mm = split3(o, w2h[:, w, :], w2l[:, w, :],
                                (hi[:, :, odd, at:at + N // 2], lo[:, :, odd, at:at + N // 2]),
                                g == 0, g == PRODUCTS[product] - 1)
                mm.then_inc(c2_mm, 1)

            def distance(pair, s, first):
                pe.wait_ge(dR_ok, after(pair, s))
                pe.wait_ge(dL_ok, after(pair, s))
                if s == 0:
                    pe.wait_ge(mb_ok, after(pair, 1))
                    pe.wait_ge(sqr_ok, after(pair, 1))
                    pe.wait_ge(slin_ok, after(pair, 1))
                    if first:
                        pe.wait_ge(h_ok, after(pair, 1))
                    else:
                        pe.wait_ge(out_ok, after(pair - 1, 0))
                else:
                    pe.wait_ge(exp_ok, after(pair, 0))
                for b in range(NB):
                    mm = nc.tensor.matmul(bank(4 + b), dL[s][:, b * P:(b + 1) * P], dR[s][:], start=True, stop=True)
                mm.then_inc(dist_mm, 1)

            def gather(pair, s):
                pe.wait_ge(em_ok, after(pair, s))
                pe.wait_ge(msg_ok, after(pair, s))
                for b in range(NB):
                    mm = nc.tensor.matmul(bank(GATHER_BANK[s]), msg[s][:, b, :], em[s][:, b, :], start=b == 0, stop=b == NB - 1)
                mm.then_inc(nm_mm, 1)

            def cols(g):
                return slice(g * D, (g + 1) * D)

            def gate(pair, par, s, g):
                if g == GATE_R:
                    pe.wait_ge(xch_ok, after(pair, s))
                    pe.wait_ge(xcl_ok, after(pair, s))
                    pe.wait_ge(nmh_ok, after(pair, s))
                    pe.wait_ge(nml_ok, after(pair, s))
                if s == 1:
                    pe.wait_ge((tr_ok, tz_ok)[g], after(pair, 0))
                split3(bank(g), whhh[:, cols(g)], whhl[:, cols(g)], (x1h[par][s], x1l[par][s]), True, False)
                split3(bank(g), wihh[:, 0, cols(g)], wihl[:, 0, cols(g)], (xch[s][:], xcl[s][:]), False, False)
                split3(bank(g), wihh[:, 1, cols(g)], wihl[:, 1, cols(g)], (nmh[s][:], nml[s][:]), False, True).then_inc((r_mm, z_mm)[g], 1)

            def gates_n(pair, par, s):
                if s == 1:
                    pe.wait_ge(q1_ok, after(pair, 0))
                split3(bank(GATE_HN), whhh[:, cols(2)], whhl[:, cols(2)], (x1h[par][s], x1l[par][s]), True, True).then_inc(hn_mm, 1)
                if s == 1:
                    pe.wait_ge(q2_ok, after(pair, 0))
                split3(bank(GATE_IN), wihh[:, 0, cols(2)], wihl[:, 0, cols(2)], (xch[s][:], xcl[s][:]), True, False)
                split3(bank(GATE_IN), wihh[:, 1, cols(2)], wihl[:, 1, cols(2)], (nmh[s][:], nml[s][:]), False, True).then_inc(in_mm, 1)

            def transpose_y1(pair, s):
                pe.wait_ge(y1_ok, after(pair, s))
                for b in range(NB):
                    mm = nc.tensor.transpose(bank(Y1_BANK[s])[:, b * P:(b + 1) * P], y1[s][:, b * P:(b + 1) * P], ident)
                mm.then_inc(y1_mm, 1)

            def body(pair, par, first=False, last=False):
                conv2(pair, 0, first)
                conv2(pair, 1, first)
                if not first:
                    pe.wait_ge(q2_ok, after(pair - 1, 1))
                    transpose_y1(pair - 1, 1)
                distance(pair, 0, first)
                conv2(pair, 2, first)
                distance(pair, 1, first)
                conv2(pair, 3, first)
                pe.wait_ge(exp_ok, after(pair, 1))
                if not last:
                    for s in range(2):
                        first_layer_in(pair + 1, s)
                gather(pair, 0)
                if not last:
                    first_layer_adj(pair + 1, 0)
                    first_layer_adj(pair + 1, 1)
                gather(pair, 1)
                if first:
                    pe.wait_ge(w_hi, GATE_WEIGHTS)
                    pe.wait_ge(w_lo, GATE_WEIGHTS)
                gate(pair, par, 0, GATE_R)
                gate(pair, par, 0, GATE_Z)
                if not last:
                    transpose_x1(pair + 1, 0)
                gates_n(pair, par, 0)
                if not last:
                    conv1(pair + 1, 1 - par, 0, False)
                    embed(pair + 1, 1 - par, 0)
                    messages(pair + 1, 1 - par, 0)
                    transpose_x1(pair + 1, 1)
                gate(pair, par, 1, GATE_R)
                if not last:
                    conv1(pair + 1, 1 - par, 1, False)
                    messages(pair + 1, 1 - par, 1)
                    embed(pair + 1, 1 - par, 1)
                gate(pair, par, 1, GATE_Z)
                gates_n(pair, par, 1)
                if not last:
                    pe.wait_ge(h_ok, after(pair + 1, 1))
                else:
                    pe.wait_ge(nml_ok, after(pair, 1))
                transpose_y1(pair, 0)

            pe.wait_ge(first_in, 16)
            for s in range(2):
                first_layer_in(0, s)
                first_layer_adj(0, s)
            transpose_x1(0, 0)
            pe.wait_ge(w_hi, X1_WEIGHTS)
            pe.wait_ge(w_lo, X1_WEIGHTS)
            pe.wait_ge(columns_in, 16)
            conv1(0, 0, 0, True)
            transpose_x1(0, 1)
            embed(0, 0, 0)
            conv1(0, 0, 1, True)
            messages(0, 0, 0)
            messages(0, 0, 1)
            embed(0, 0, 1)
            pair_loop(pe, body)
            transpose_y1(PAIRS - 1, 1)

        @block.scalar
        def _(act):
            def scaled_blocks(out_, src, rs, sh):
                for b in range(NB):
                    i = nc.scalar.activation(out_[:, b, :], src[:, b, :], ACT.Identity, bias=sh[:, b:b + 1], scale=rs[:, b:b + 1])
                return i

            def degree(pair, s):
                act.wait_ge(adjN_in, (pair * 2 + (s + 1)) * 16)
                for b in range(NB):
                    i = nc.scalar.activation(adjN[:, b, :], adjN[:, b, :], ACT.Copy, accum_out=deg[s][:, b:b + 1])
                i.then_inc(deg_ok, 1)

            def weights_hi(start, stop):
                for dst, src, factor in weight_halves[start:stop]:
                    nc.scalar.activation(dst[0], src, ACT.Copy, scale=factor).then_inc(w_hi, 1)

            def x1_norm(pair, s):
                act.wait_ge(shift_ok, after(pair, s))
                scaled_blocks(x1N[s], y0[s], rstd[s], shift[s]).then_inc(x1N_ok, 1)

            def x1_out(pair, par, s, reuse):
                act.wait_ge(x1_mm, after(pair, s))
                if reuse:
                    act.wait_ge(y1_ok, after(pair - 2, s))
                nc.scalar.activation(x1T[par][s], bank(X1_BANK[s]), ACT.Copy).then_inc(x1T_ok, 1)
                nc.scalar.activation(x1h[par][s], bank(X1_BANK[s]), ACT.Copy).then_inc(x1h_ok, 1)

            def conv1_out(pair, s, first):
                act.wait_ge(c1_mm, after(pair, s))
                if not first:
                    act.wait_ge(sum1_ok, after(pair - 1, s))
                    act.wait_ge(diff1_ok, after(pair - 1, s))
                    act.wait_ge(diff2_ok, after(pair - 1, s))
                nc.scalar.activation(hT[s][:, HALO:HALO + N], bank(CONV1_BANK), ACT.Relu, bias=bn_fac[:, 1:2],
                                     scale=bn_fac[:, 0:1]).then_inc(h_ok, 1)

            def window_hi(pair, s, src, dst, src_ok, dst_ok, first):
                act.wait_ge(src_ok, after(pair, s))
                if not first:
                    act.wait_ge(c2_mm, of_pair(pair - 1, 3, 4))
                nc.scalar.activation(dst[:, s].rearrange("p e i -> p i e"), src.rearrange("p (i e) -> p i e", e=2),
                                     ACT.Copy).then_inc(dst_ok, 1)

            def embed_out(pair, s, first):
                act.wait_ge(s_mm, after(pair, s))
                if not first:
                    act.wait_ge(dL_ok, after(pair - 1, s))
                nc.scalar.activation(sqr[s][:], bank(EMBED_BANK), ACT.Square, bias=bse_col[:, 0:1]).then_inc(sqr_ok, 1)
                nc.scalar.activation(slin[s][:], bank(EMBED_BANK), ACT.Identity, bias=bse_lin[:, 0:1], scale=coef[:, 1:2]).then_inc(slin_ok, 1)

            def message_out(pair, s):
                act.wait_ge(mb_ok, after(pair, s))
                nc.scalar.activation(msg[s][:], mb_[s][:], ACT.Relu).then_inc(msg_ok, 1)

            def out_norm(pair, s, last):
                act.wait_ge(shift1_ok, after(pair, s))
                if last:
                    act.wait_ge(out_stored[s], loaded(pair - 1))
                else:
                    act.wait_ge(z1_ok, after(pair + 1, s))
                scaled_blocks(outN[s], bank(Y1_BANK[s]).rearrange("p (b d) -> p b d", b=NB), rstd1[s], shift1[s]).then_inc(out_ok, 1)

            def exps(pair, s, first):
                act.wait_ge(dist_mm, after(pair, s))
                if not first:
                    act.wait_ge(nm_mm, after(pair - 1, s))
                nc.scalar.activation(em[s].rearrange("p a b -> p (a b)"), ps[:, 4:8, :].rearrange("p a b -> p (a b)"),
                                     ACT.Exp).then_inc(exp_ok, 1)

            def conv2_out(pair, s, first):
                act.wait_ge(gc_step, of_pair(pair, 5, 6))
                if not first:
                    act.wait_ge(in_mm, after(pair - 1, s))
                nc.scalar.activation(xch[s][:], gc[s], ACT.Relu, bias=bn_fac[:, 3:4]).then_inc(xch_ok, 1)
                nc.scalar.activation(xcT[s], gc[s], ACT.Relu, bias=bn_fac[:, 3:4]).then_inc(xc_ok, 1)

            def gather_out(pair, s):
                act.wait_ge(nm_mm, after(pair, s))
                nc.scalar.activation(nmh[s][:], bank(GATHER_BANK[s]), ACT.Copy).then_inc(nmh_ok, 1)

            def gate_r_out(pair, s, first):
                act.wait_ge(r_mm, after(pair, s))
                if not first:
                    act.wait_ge(y1_ok, after(pair - 1, s))
                nc.scalar.activation(tr[s], bank(GATE_R), ACT.Tanh, bias=gbias[:, 0:1], scale=0.5).then_inc(tr_ok, 1)

            def gate_z_out(pair, s):
                act.wait_ge(z_mm, after(pair, s))
                nc.scalar.activation(tz[s], bank(GATE_Z), ACT.Tanh, bias=gbias[:, 1:2], scale=0.5).then_inc(tz_ok, 1)

            def new_state(pair, s):
                act.wait_ge(q2_ok, after(pair, s))
                nc.scalar.activation(nT[s], q2[s], ACT.Tanh, bias=bih[:, 2:3]).then_inc(n_ok, 1)

            def body(pair, par, first=False, last=False):
                if not last:
                    degree(pair + 1, 0)
                if not first:
                    out_norm(pair - 1, 0, False)
                message_out(pair, 1)
                exps(pair, 0, first)
                if not first:
                    out_norm(pair - 1, 1, False)
                exps(pair, 1, first)
                if not last:
                    degree(pair + 1, 1)
                conv2_out(pair, 0, first)
                conv2_out(pair, 1, first)
                gather_out(pair, 0)
                if not last:
                    x1_norm(pair + 1, 0)
                gather_out(pair, 1)
                gate_r_out(pair, 0, first)
                if not last:
                    x1_out(pair + 1, 1 - par, 0, not first)
                gate_z_out(pair, 0)
                if not last:
                    x1_norm(pair + 1, 1)
                new_state(pair, 0)
                if not last:
                    x1_out(pair + 1, 1 - par, 1, not first)
                    conv1_out(pair + 1, 0, False)
                    embed_out(pair + 1, 0, False)
                    window_hi(pair + 1, 0, diff2[0][:], diff2h, diff2_ok, diff2h_ok, False)
                gate_r_out(pair, 1, first)
                if not last:
                    conv1_out(pair + 1, 1, False)
                    embed_out(pair + 1, 1, False)
                    window_hi(pair + 1, 1, diff2[1][:], diff2h, diff2_ok, diff2h_ok, False)
                    message_out(pair + 1, 0)
                gate_z_out(pair, 1)
                if not last:
                    window_hi(pair + 1, 0, sum1[0][:], sum1h, sum1_ok, sum1h_ok, False)
                    window_hi(pair + 1, 0, diff1[0][:], diff1h, diff1_ok, diff1h_ok, False)
                    window_hi(pair + 1, 1, sum1[1][:], sum1h, sum1_ok, sum1h_ok, False)
                    window_hi(pair + 1, 1, diff1[1][:], diff1h, diff1_ok, diff1h_ok, False)
                new_state(pair, 1)

            degree(0, 0)
            degree(0, 1)
            act.wait_ge(staged_in, 16)
            act.wait_ge(wse_ok, 1)
            weights_hi(0, X1_WEIGHTS)
            x1_norm(0, 0)
            x1_out(0, 0, 0, False)
            act.wait_ge(taps_in, 16)
            act.wait_ge(tap_zero, 1)
            weights_hi(X1_WEIGHTS, X1_WEIGHTS + 1)
            act.wait_ge(fold_ok, 1)
            act.wait_ge(halo_ok, 2)
            act.wait_ge(bse_in, 16)
            x1_norm(0, 1)
            conv1_out(0, 0, True)
            x1_out(0, 0, 1, False)
            embed_out(0, 0, True)
            act.wait_ge(taps_step, 3)
            weights_hi(X1_WEIGHTS + 1, X1_WEIGHTS + 2)
            conv1_out(0, 1, True)
            window_hi(0, 0, diff2[0][:], diff2h, diff2_ok, diff2h_ok, True)
            window_hi(0, 1, diff2[1][:], diff2h, diff2_ok, diff2h_ok, True)
            embed_out(0, 1, True)
            message_out(0, 0)
            for s in range(2):
                window_hi(0, s, sum1[s][:], sum1h, sum1_ok, sum1h_ok, True)
                window_hi(0, s, diff1[s][:], diff1h, diff1_ok, diff1h_ok, True)
            weights_hi(X1_WEIGHTS + 2, GATE_WEIGHTS)
            pair_loop(act, body)
            for s in range(2):
                out_norm(PAIRS - 1, s, True)

        @block.vector
        def _(dve):
            def blocks(x):
                return x.rearrange("p (b d) -> p b d", b=NB)

            def norm(pair, s, src, m, st, rs, mv_ok, var_ok):
                for b in range(NB):
                    nc.vector.bn_stats(st[s][:, b, :], src[:, b, :])
                dve.drain()
                for b in range(NB):
                    i = nc.vector.bn_aggr(m[s][:, b, :], st[s][:, b, :])
                i.then_inc(mv_ok, 1)
                dve.wait_ge(mv_ok, after(pair, s))
                nc.vector.tensor_scalar(rs[s][:], m[s][:, :, 1], EPS, None, ALU.add).then_inc(var_ok, 1)

            def norm_shift(pair, s, m, rs, sh, rstd_ok, shift_ok):
                dve.wait_ge(rstd_ok, after(pair, s))
                nc.vector.scalar_tensor_tensor(sh[s][:], m[s][:, :, 0], -1.0, rs[s][:], ALU.mult, ALU.mult).then_inc(shift_ok, 1)

            def degree(pair, s):
                dve.wait_ge(deg_ok, after(pair, s))
                nc.vector.tensor_scalar(deg[s][:], deg[s][:], 1.0, None, ALU.add).then_inc(deg1_ok, 1)

            def scale_in(pair, s, reuse):
                dve.wait_ge(dinv_ok, after(pair, s))
                dve.wait_ge(y_mm, after(pair, s))
                if reuse:
                    dve.wait_ge(out_stored[s], loaded(pair - 2))
                nc.vector.tensor_tensor(yd[s][:], blocks(bank(Y_BANK[s])), dinv[s][:].unsqueeze(2).to_broadcast([P, NB, D]),
                                        ALU.mult).then_inc(yd_ok, 1)

            def first_layer_out(pair, s):
                dve.wait_ge(l0_mm, after(pair, s))
                nc.vector.tensor_tensor(z1[s][:], blocks(bank(ADJ_BANK[s])), yd[s][:], ALU.add).then_inc(z1_ok, 1)

            def first_layer_sum(pair, s):
                dve.wait_ge(z3_ok, after(pair, s))
                dve.wait_ge(xN_in[s], loaded(pair))
                nc.vector.scalar_tensor_tensor(y0[s][:].rearrange("p b d -> p (b d)"), z3[s][:].rearrange("p b d -> p (b d)"), 0.0,
                                               xN[s][:].rearrange("p b d -> p (b d)"), ALU.max, ALU.add).then_inc(y0_ok, 1)

            def first_layer_norm(pair, s):
                dve.wait_ge(y0_ok, after(pair, s))
                norm(pair, s, y0[s], mv, stats, rstd, mv_ok, var_ok)

            def x1_lo(pair, par, s):
                dve.wait_ge(x1h_ok, after(pair, s))
                dve.wait_ge(x1T_ok, after(pair, s))
                nc.vector.tensor_tensor(x1l[par][s], x1T[par][s], x1h[par][s].bitcast(FP32), ALU.subtract).then_inc(x1l_ok, 1)

            def window_diff2(pair, s):
                dve.wait_ge(h_ok, after(pair, s))
                nc.vector.tensor_tensor(diff2[s][:], hT[s][:, 0:WIN], hT[s][:, 2:WIN + 2], ALU.subtract).then_inc(diff2_ok, 1)

            def window_lo(pair, s, src, hi, lo, hi_ok, lo_ok):
                dve.wait_ge(hi_ok, after(pair, s))
                nc.vector.tensor_tensor(lo[:, s].rearrange("p e i -> p i e"), src.rearrange("p (i e) -> p i e", e=2),
                                        hi[:, s].bitcast(FP32).rearrange("p e i -> p i e"), ALU.subtract).then_inc(lo_ok, 1)

            def dist_rows(pair, s):
                dve.wait_ge(sqr_ok, after(pair, s))
                dve.wait_ge(slin_ok, after(pair, s))
                nc.vector.scalar_tensor_tensor(su[s][:], sqr[s][:], coef[:, 0:1], slin[s][:], ALU.mult, ALU.add).then_inc(su_ok, 1)
                dve.wait_ge(su_ok, after(pair, s))
                nc.vector.tensor_copy(suh[:], su[s][:]).then_inc(suh_ok, 1)

            def dist_sides(pair, s):
                nc.vector.tensor_scalar(suR[s][:], su[s][:], coef[:, 3:4], coef[:, 4:5], ALU.mult, ALU.add).then_inc(suR_ok, 1)
                nc.vector.tensor_scalar(suL[s][:], su[s][:], coef[:, 6:7], coef[:, 7:8], ALU.mult, ALU.add).then_inc(suL_ok, 1)

            def dist_operands(pair, s):
                dve.wait_ge(suh_ok, after(pair, s))
                dve.wait_ge(suR_ok, after(pair, s))
                nc.vector.scalar_tensor_tensor(dR[s][:], suh[:].bitcast(FP32), coef[:, 2:3], suR[s][:], ALU.mult, ALU.add).then_inc(dR_ok, 1)
                dve.wait_ge(suL_ok, after(pair, s))
                nc.vector.scalar_tensor_tensor(dL[s][:], suh[:].bitcast(FP32), coef[:, 5:6], suL[s][:], ALU.mult, ALU.add).then_inc(dL_ok, 1)

            def message_out(pair, s, first):
                dve.wait_ge(msg_mm, after(pair, s))
                if not first:
                    dve.wait_ge(nm_mm, after(pair - 1, s))
                nc.vector.tensor_tensor(mb_[s][:], blocks(bank(MSG_BANK[s])), bmsg_rep[:].unsqueeze(1).to_broadcast([P, NB, D]),
                                        ALU.add).then_inc(mb_ok, 1)

            def mask(pair, s):
                dve.wait_ge(exp_ok, after(pair, s))
                nc.vector.tensor_tensor(em[s], em[s], adjT[s][:], ALU.mult).then_inc(em_ok, 1)

            def half(v, odd):
                return v.rearrange("p s (t e) -> p s t e", e=2)[:, :, :, odd]

            def combine(pair, par, step, first):
                product, odd, factor, before = ((1, 0, bn_fac[:, 2:3], None), (1, 1, bn_fac[:, 2:3], None), (2, 0, bn_fac[:, 2:3], 0),
                                                (2, 1, bn_minus[:], 1), (0, 0, bn_fac[:, 2:3], 2), (3, 1, bn_fac[:, 2:3], 3))[step]
                dve.wait_ge(c2_mm, of_pair(pair, product, 4))
                if before is not None:
                    dve.wait_ge(gc_step, of_pair(pair, before, 6))
                elif step == 0 and not first:
                    dve.wait_ge(xcl_ok, after(pair - 1, 1))
                added = x1T_pair[par][:] if before is None else gc_pair[:]
                nc.vector.scalar_tensor_tensor(half(gc_pair[:], odd), bank(product).rearrange("p (s t) -> p s t", s=2), factor,
                                               half(added, odd), ALU.mult, ALU.add).then_inc(gc_step, 1)

            def xc_lo(pair, s):
                dve.wait_ge(xc_ok, after(pair, s))
                dve.wait_ge(xch_ok, after(pair, s))
                nc.vector.tensor_tensor(xcl[s][:], xcT[s], xch[s][:].bitcast(FP32), ALU.subtract).then_inc(xcl_ok, 1)

            def nm_lo(pair, s):
                dve.wait_ge(nmh_ok, after(pair, s))
                nc.vector.tensor_tensor(nml[s][:], bank(GATHER_BANK[s]), nmh[s][:].bitcast(FP32), ALU.subtract).then_inc(nml_ok, 1)

            def gate_r_out(pair, s):
                dve.wait_ge(tr_ok, after(pair, s))
                nc.vector.tensor_scalar(tr1[s], tr[s], 1.0, 0.5, ALU.add, ALU.mult).then_inc(tr1_ok, 1)

            def new_state_in(pair, s):
                dve.wait_ge(tr1_ok, after(pair, s))
                dve.wait_ge(hn_mm, after(pair, s))
                nc.vector.scalar_tensor_tensor(q1[s], bank(GATE_HN), bhh[:, 2:3], tr1[s], ALU.add, ALU.mult).then_inc(q1_ok, 1)
                dve.wait_ge(q1_ok, after(pair, s))
                dve.wait_ge(in_mm, after(pair, s))
                nc.vector.tensor_tensor(q2[s], bank(GATE_IN), q1[s], ALU.add).then_inc(q2_ok, 1)

            def state_factor(pair, s):
                dve.wait_ge(tz_ok, after(pair, s))
                nc.vector.tensor_scalar(kept_factor[s], tz[s], 0.5, 1.5, ALU.mult, ALU.add).then_inc(factor_ok, 1)

            def state_out(pair, s):
                dve.wait_ge(n_ok, after(pair, s))
                nc.vector.scalar_tensor_tensor(minus_new[s], tz[s], 1.0, nT[s], ALU.subtract, ALU.mult).then_inc(minus_ok, 1)
                dve.wait_ge(minus_ok, after(pair, s))
                dve.wait_ge(kept_ok, after(pair, s))
                nc.vector.scalar_tensor_tensor(y1[s], minus_new[s], -0.5, kept[s], ALU.mult, ALU.add).then_inc(y1_ok, 1)

            def second_norm(pair, s):
                dve.wait_ge(y1_mm, after(pair, s))
                norm(pair, s, blocks(bank(Y1_BANK[s])), mv1, stats1, rstd1, mv1_ok, var1_ok)

            def second_shift(pair, s):
                norm_shift(pair, s, mv1, rstd1, shift1, rstd1_ok, shift1_ok)

            def first_shift(pair, s):
                norm_shift(pair, s, mv, rstd, shift, rstd_ok, shift_ok)

            def body(pair, par, first=False, last=False):
                if not first:
                    second_norm(pair - 1, 0)
                dist_operands(pair, 0)
                if not first:
                    second_shift(pair - 1, 0)
                    state_out(pair - 1, 1)
                message_out(pair, 1, first)
                dist_rows(pair, 1)
                if not first:
                    second_norm(pair - 1, 1)
                dist_sides(pair, 1)
                if not first:
                    second_shift(pair - 1, 1)
                dist_operands(pair, 1)
                if first:
                    weights_lo(CONV2_WEIGHTS, GATE_WEIGHTS)
                combine(pair, par, 0, first)
                combine(pair, par, 1, first)
                if not last:
                    degree(pair + 1, 0)
                mask(pair, 0)
                combine(pair, par, 2, first)
                combine(pair, par, 3, first)
                combine(pair, par, 4, first)
                if last:
                    combine(pair, par, 5, first)
                mask(pair, 1)
                if not last:
                    combine(pair, par, 5, first)
                if not last:
                    scale_in(pair + 1, 0, not first)
                    degree(pair + 1, 1)
                xc_lo(pair, 0)
                xc_lo(pair, 1)
                if not last:
                    scale_in(pair + 1, 1, not first)
                nm_lo(pair, 0)
                if not last:
                    first_layer_out(pair + 1, 0)
                    first_layer_sum(pair + 1, 0)
                    first_layer_out(pair + 1, 1)
                    first_layer_norm(pair + 1, 0)
                    first_shift(pair + 1, 0)
                nm_lo(pair, 1)
                if not last:
                    first_layer_sum(pair + 1, 1)
                    first_layer_norm(pair + 1, 1)
                    x1_lo(pair + 1, 1 - par, 0)
                gate_r_out(pair, 0)
                if not last:
                    first_shift(pair + 1, 1)
                state_factor(pair, 0)
                new_state_in(pair, 0)
                if not last:
                    x1_lo(pair + 1, 1 - par, 1)
                    window_diff2(pair + 1, 0)
                state_out(pair, 0)
                if not last:
                    message_out(pair + 1, 0, False)
                    window_lo(pair + 1, 0, diff2[0][:], diff2h, diff2l, diff2h_ok, diff2l_ok)
                    window_diff2(pair + 1, 1)
                    dist_rows(pair + 1, 0)
                    dist_sides(pair + 1, 0)
                    window_lo(pair + 1, 1, diff2[1][:], diff2h, diff2l, diff2h_ok, diff2l_ok)
                gate_r_out(pair, 1)
                state_factor(pair, 1)
                if not last:
                    window_lo(pair + 1, 0, sum1[0][:], sum1h, sum1l, sum1h_ok, sum1l_ok)
                new_state_in(pair, 1)
                if not last:
                    window_lo(pair + 1, 1, sum1[1][:], sum1h, sum1l, sum1h_ok, sum1l_ok)

            bn4 = bn.rearrange("p (l k) -> p k l", l=2)
            fac = bn_fac[:].rearrange("p (l k) -> p k l", l=2)

            def small_weights():
                dve.wait_ge(columns_in, 16)
                nc.vector.tensor_copy(wse_rep[:, 0:DIST_ROWS].rearrange("p (a b) -> p a b", b=SE),
                                      wseT.unsqueeze(1).to_broadcast([P, DIST_ROWS // SE, SE])).then_inc(wse_ok, 1)
                nc.vector.tensor_scalar(bn_tmp[:, 0:2], bn4[:, 3, :], EPS, None, ALU.add).then_inc(fold_var, 1)
                nc.vector.tensor_tensor(gbias2[:, 0:2], bih[:, 0:2], bhh[:, 0:2], ALU.add).then_inc(fold_step, 1)

            def small_weights_folded():
                dve.wait_ge(fold_step, 1)
                nc.vector.tensor_scalar(gbias[:, 0:2], gbias2[:, 0:2], 0.5, None, ALU.mult).then_inc(fold_step, 1)
                dve.wait_ge(fold_pow, 1)
                nc.vector.tensor_tensor(fac[:, 0, :], bn4[:, 0, :], bn_tmp[:, 0:2], ALU.mult).then_inc(fold_step, 1)
                dve.wait_ge(fold_step, 3)
                nc.vector.tensor_tensor(bn_tmp[:, 2:4], bn4[:, 2, :], fac[:, 0, :], ALU.mult).then_inc(fold_step, 1)
                nc.vector.tensor_scalar(bn_minus[:], bn_fac[:, 2:3], -1.0, None, ALU.mult).then_inc(fold_step, 1)
                dve.wait_ge(fold_step, 5)
                nc.vector.tensor_tensor(fac[:, 1, :], bn4[:, 1, :], bn_tmp[:, 2:4], ALU.subtract).then_inc(fold_step, 1)
                dve.wait_ge(bse_in, 16)
                nc.vector.tensor_tensor(bse_lin[:], bse_col[:], coef[:, 1:2], ALU.mult).then_inc(fold_ok, 1)

            def tap_sums():
                dve.wait_ge(taps_in, 16)
                dve.wait_ge(tap_zero, 1)
                nc.vector.tensor_tensor(w2_plus, w2[:, 0::3, :], w2[:, 2::3, :], ALU.add).then_inc(taps_step, 1)
                dve.wait_ge(taps_step, 1)
                nc.vector.tensor_tensor(w2_minus, w2_plus, w2[:, 1::3, :], ALU.subtract).then_inc(taps_step, 1)
                dve.wait_ge(taps_step, 2)
                nc.vector.tensor_tensor(w2_plus, w2_plus, w2[:, 1::3, :], ALU.add).then_inc(taps_step, 1)

            def weights_lo(start, stop):
                for i, ((hi, lo), whole, factor) in enumerate(weight_halves[start:stop]):
                    dve.wait_ge(w_hi, start + i + 1)
                    nc.vector.scalar_tensor_tensor(lo, whole, factor, hi.bitcast(FP32), ALU.mult, ALU.subtract).then_inc(w_lo, 1)

            nc.vector.memset(wse_rep[:], 0.0)
            degree(0, 0)
            scale_in(0, 0, False)
            degree(0, 1)
            first_layer_out(0, 0)
            scale_in(0, 1, False)
            small_weights()
            first_layer_sum(0, 0)
            first_layer_norm(0, 0)
            first_layer_out(0, 1)
            small_weights_folded()
            first_shift(0, 0)
            weights_lo(0, X1_WEIGHTS)
            first_layer_sum(0, 1)
            first_layer_norm(0, 1)
            x1_lo(0, 0, 0)
            first_shift(0, 1)
            tap_sums()
            window_diff2(0, 0)
            x1_lo(0, 0, 1)
            weights_lo(X1_WEIGHTS, X1_WEIGHTS + 2)
            window_lo(0, 0, diff2[0][:], diff2h, diff2l, diff2h_ok, diff2l_ok)
            window_diff2(0, 1)
            dist_rows(0, 0)
            window_lo(0, 1, diff2[1][:], diff2h, diff2l, diff2h_ok, diff2l_ok)
            dve.wait_ge(bmsg_in, 16)
            message_out(0, 0, True)
            dist_sides(0, 0)
            for s in range(2):
                window_lo(0, s, sum1[s][:], sum1h, sum1l, sum1h_ok, sum1l_ok)
            weights_lo(X1_WEIGHTS + 2, CONV2_WEIGHTS)
            pair_loop(dve, body)
            second_norm(PAIRS - 1, 0)
            state_out(PAIRS - 1, 1)
            second_shift(PAIRS - 1, 0)
            second_norm(PAIRS - 1, 1)
            second_shift(PAIRS - 1, 1)

        @block.gpsimd
        def _(pool):
            def rsqrt(tile, ready, done):
                pool.wait_ge(*ready)
                nc.gpsimd.tensor_tensor(tile, tile, neg_half[:, 0:tile.shape[1]], ALU.pow).then_inc(done, 1)

            def degrees(pair, s):
                pool.wait_ge(deg1_ok, after(pair, s))
                nc.gpsimd.tensor_tensor(dinv[s][:], deg[s][:], neg_half[:], ALU.pow).then_inc(dinv_ok, 1)

            def first_layer_scale(pair, s):
                pool.wait_ge(z1_ok, after(pair, s))
                nc.gpsimd.tensor_tensor(z2[s][:], z1[s][:], dinv[s][:].unsqueeze(2).to_broadcast([P, NB, D]), ALU.mult).then_inc(z2_ok, 1)

            def first_layer_bias(pair, s):
                pool.wait_ge(z2_ok, after(pair, s))
                nc.gpsimd.tensor_tensor(z3[s][:], z2[s][:], b0_rep[:].unsqueeze(1).to_broadcast([P, NB, D]), ALU.add).then_inc(z3_ok, 1)

            def first_rsqrt(pair, s):
                rsqrt(rstd[s][:], (var_ok, after(pair, s)), rstd_ok)

            def second_rsqrt(pair, s):
                rsqrt(rstd1[s][:], (var1_ok, after(pair, s)), rstd1_ok)

            def windows(pair, s, kind, first):
                pool.wait_ge(h_ok, after(pair, s))
                if kind == "sum1":
                    if not first:
                        pool.wait_ge(sum1l_ok, after(pair - 1, s))
                    nc.gpsimd.tensor_tensor(sum1[s][:], hT[s][:, 0:WIN], hT[s][:, 1:WIN + 1], ALU.add).then_inc(sum1_ok, 1)
                else:
                    nc.gpsimd.tensor_tensor(diff1[s][:], hT[s][:, 1:WIN + 1], hT[s][:, 0:WIN], ALU.subtract).then_inc(diff1_ok, 1)

            def diff1_lo(pair, s):
                pool.wait_ge(diff1h_ok, after(pair, s))
                nc.gpsimd.tensor_tensor(diff1l[:, s].rearrange("p e i -> p i e"), diff1[s][:].rearrange("p (i e) -> p i e", e=2),
                                        diff1h[:, s].bitcast(FP32).rearrange("p e i -> p i e"), ALU.subtract).then_inc(diff1l_ok, 1)

            def state_kept(pair, s, par):
                pool.wait_ge(factor_ok, after(pair, s))
                nc.gpsimd.tensor_tensor(kept[s], kept_factor[s], x1T[par][s], ALU.mult).then_inc(kept_ok, 1)

            def body(pair, par, first=False, last=False):
                diff1_lo(pair, 0)
                if not first:
                    state_kept(pair - 1, 1, 1 - par)
                    second_rsqrt(pair - 1, 0)
                diff1_lo(pair, 1)
                if not first:
                    second_rsqrt(pair - 1, 1)
                if not last:
                    for s in range(2):
                        degrees(pair + 1, s)
                    first_layer_scale(pair + 1, 0)
                    first_layer_bias(pair + 1, 0)
                    first_layer_scale(pair + 1, 1)
                    first_rsqrt(pair + 1, 0)
                    first_layer_bias(pair + 1, 1)
                    first_rsqrt(pair + 1, 1)
                state_kept(pair, 0, par)
                if not last:
                    windows(pair + 1, 0, "sum1", False)
                    windows(pair + 1, 0, "diff1", False)
                    windows(pair + 1, 1, "sum1", False)
                    windows(pair + 1, 1, "diff1", False)

            nc.gpsimd.memset(bse_col[:], 0.0).then_inc(bse_zero, 1)
            nc.gpsimd.memset(w2[:, TAPS:, :], 0.0).then_inc(tap_zero, 1)
            nc.gpsimd.memset(neg_half[:], -0.5).then_inc(half_ok, 1)
            for tile in hT:
                nc.gpsimd.memset(tile[:, 0:HALO], 0.0)
                nc.gpsimd.memset(tile[:, HALO + N:PADDED], 0.0).then_inc(halo_ok, 1)
            pool.wait_ge(half_ok, 1)
            degrees(0, 0)
            degrees(0, 1)
            pool.wait_ge(b0_in, 16)
            first_layer_scale(0, 0)
            first_layer_bias(0, 0)
            rsqrt(bn_tmp[:, 0:2], (fold_var, 1), fold_pow)
            first_rsqrt(0, 0)
            first_layer_scale(0, 1)
            first_layer_bias(0, 1)
            first_rsqrt(0, 1)
            windows(0, 0, "sum1", True)
            windows(0, 0, "diff1", True)
            windows(0, 1, "sum1", True)
            windows(0, 1, "diff1", True)
            pair_loop(pool, body)
            state_kept(PAIRS - 1, 1, 1)
            for s in range(2):
                second_rsqrt(PAIRS - 1, s)


def kernel(**inputs):
    import numpy as np
    from concourse import bacc
    from concourse.bass_utils import run_bass_kernel_spmd

    a = {k: np.asarray(v) for k, v in inputs.items()}
    L = {k[len("L1_gnn_"):]: v for k, v in a.items() if k.startswith("L1_gnn_")}
    arrays = {
        "adjN": a["adj"], "adjT": a["adj"].transpose(0, 2, 1), "xN": a["x"], "xT": a["x"].transpose(0, 2, 1),
        "first_weights": np.concatenate([a["L0_gnn_W"].T, np.eye(P, dtype=np.float32)], axis=1),
        "columns": np.concatenate([
            L["w_msg"].T, L["w_se"].T, distance_factors(), L["b_ih"].reshape(3, D).T, L["b_hh"].reshape(3, D).T,
            np.stack([L[f"bn{i}_{k}"] for i in (1, 2) for k in "gbmv"], axis=1)], axis=1),
        "staged": np.concatenate([L["w_ih"].T[0:P], L["w_ih"].T[P:2 * P], L["w_hh"].T, L["conv1_w"][:, :, 0].T], axis=1),
        "w2T": L["conv2_w"].transpose(1, 2, 0), "b0": a["L0_gnn_b"], "bmsg": L["b_msg"],
        "bse": np.tile(L["b_se"], DIST_ROWS // SE)[:, None],
    }
    arrays = {f"in_{k}": np.ascontiguousarray(v) for k, v in arrays.items()}
    nc = bacc.Bacc("TRN2", target_bir_lowering=False, num_devices=1)
    t = {k[3:]: nc.dram_tensor(k, v.shape, mybir.dt.from_np(v.dtype), kind="ExternalInput").ap() for k, v in arrays.items()}
    out = nc.dram_tensor("out", (G, N, D), FP32, kind="ExternalOutput").ap()
    gnn_kernel(nc, t, out)
    r = run_bass_kernel_spmd(nc, [arrays], core_ids=[0])
    return r.results[0]["out"]
```
